# Optimizing a Trainium2 kernel written in Bass

```python
import numpy as np
import jax
import jax.numpy as jnp

def _softmax(x, axis=-1):
    return jax.nn.softmax(x, axis=axis)

def _gelu(x):
    return jax.nn.gelu(x, approximate=True)

def _silu(x):
    return jax.nn.silu(x)

def _sigmoid(x):
    return jax.nn.sigmoid(x)

def _layernorm(x, axis=-1, eps=1e-05):
    m = jnp.mean(x, axis=axis, keepdims=True)
    v = jnp.var(x, axis=axis, keepdims=True)
    return (x - m) / jnp.sqrt(v + eps)

def _scatter_add(tgt, idx, src, axis=0):
    return tgt.at[idx].add(src)

def _segment_sum(src, seg, n):
    return jax.ops.segment_sum(src, seg, n)
kernel_name = 'mk_decoder_postln_d1_seqx_r8_17ec0c'

def setup_inputs(seed: int=0):
    np.random.seed(seed)
    _w = jnp.asarray

    def _rec_inputs():
        import jax
        import jax.numpy as jnp
        _rk = jax.random.key(seed)
        x = 7.22e-05 + 1 * jax.random.normal(jax.random.fold_in(_rk, 1), (16, 56, 256), jnp.float32)
        _lenS = 56 - jax.random.randint(jax.random.fold_in(_rk, 7), (16,), 0, max(1, 56 // 4) + 1, jnp.int32)
        _lenS2 = 1500 - jax.random.randint(jax.random.fold_in(_rk, 8), (16,), 0, max(1, 1500 // 4) + 1, jnp.int32)
        _ctx_512P = jax.random.normal(jax.random.fold_in(_rk, 11), (16, 16, 64), jnp.float32)
        _ctx_512c = jax.random.dirichlet(jax.random.fold_in(_rk, 511), 0.3 * jnp.ones((16,), jnp.float32), (16, 1500))
        _ctx_512t = jnp.einsum('bsk,bkd->bsd', _ctx_512c, _ctx_512P)
        _ctx_512t = _ctx_512t * jax.lax.rsqrt(jnp.mean(jnp.square(_ctx_512t)) + 1e-12) * 0.953939
        ctx_512 = -0.000514642 + 1.00011 * (_ctx_512t + 0.3 * jax.random.normal(jax.random.fold_in(_rk, 611), (16, 1500, 64), jnp.float32))
        return (x, ctx_512)
    x, ctx_512 = _rec_inputs()

    def _L0_attn_setup():
        import jax, jax.numpy as jnp
        import numpy as np
        import math
        D_MODEL = 256
        N_HEADS = 16
        D_HEAD = 128
        BATCH = 2
        SEQ = 256
        key = jax.random.key(seed)
        ks = jax.random.split(key, 5)
        std = 0.02
        x = jax.random.normal(ks[0], (BATCH, SEQ, D_MODEL), dtype=jnp.float32)
        W_Q = std * jax.random.normal(ks[1], (N_HEADS, D_HEAD, D_MODEL), dtype=jnp.float32)
        W_K = std * jax.random.normal(ks[2], (N_HEADS, D_HEAD, D_MODEL), dtype=jnp.float32)
        W_V = std * jax.random.normal(ks[3], (N_HEADS, D_HEAD, D_MODEL), dtype=jnp.float32)
        W_O = std * jax.random.normal(ks[4], (N_HEADS, D_MODEL, D_HEAD), dtype=jnp.float32)
        return {'x': x, 'W_Q': W_Q, 'W_K': W_K, 'W_V': W_V, 'W_O': W_O}
    _L0_attn_all = _L0_attn_setup()
    _L0_attn_in = {k: v for k, v in _L0_attn_all.items() if k in ('W_Q', 'W_K', 'W_V', 'W_O')}
    del _L0_attn_all

    def _L0_xattn_setup():
        import jax, jax.numpy as jnp
        import numpy as np
        B, S, H, NH, L = (2, 256, 256, 16, 64)
        HD = H // NH
        key = jax.random.key(seed)
        k1, k2, k3, k4, k5 = jax.random.split(key, 5)
        scale = 0.02
        return {'q': jax.random.normal(k1, (B, S, H), dtype=jnp.float32), 'latent_kv': jax.random.normal(k2, (B, S, L), dtype=jnp.float32), 'Wq': jax.random.normal(k3, (H, H), dtype=jnp.float32) * scale, 'Wkv_expand': jax.random.normal(k4, (2 * H, L), dtype=jnp.float32) * scale, 'Wout': jax.random.normal(k5, (H, H), dtype=jnp.float32) * scale}
    _L0_xattn_all = _L0_xattn_setup()
    _L0_xattn_in = {k: v for k, v in _L0_xattn_all.items() if k in ('Wq', 'Wkv_expand', 'Wout')}
    del _L0_xattn_all

    def _L0_ffn_setup():
        import jax, jax.numpy as jnp
        import numpy as np
        B, S, D, K, R = (4, 256, 256, 8, 64)
        key = jax.random.key(seed)
        ks = jax.random.split(key, 7)
        x = jax.random.normal(ks[0], (B, S, D), dtype=jnp.float32)
        U = jax.random.normal(ks[1], (K, D, R), dtype=jnp.float32) * 0.02
        V = jax.random.normal(ks[2], (K, R, D), dtype=jnp.float32) * 0.02
        W1 = jax.random.normal(ks[3], (D, D), dtype=jnp.float32) * 0.02
        b1 = jnp.zeros((D,), dtype=jnp.float32)
        W2 = jax.random.normal(ks[4], (D, K), dtype=jnp.float32) * 0.02
        b2 = jnp.zeros((K,), dtype=jnp.float32)
        return {'x': x, 'U': U, 'V': V, 'W1': W1, 'b1': b1, 'W2': W2, 'b2': b2}
    _L0_ffn_all = _L0_ffn_setup()
    _L0_ffn_in = {k: v for k, v in _L0_ffn_all.items() if k in ('U', 'V', 'W1', 'b1', 'W2', 'b2')}
    del _L0_ffn_all
    return {'x': x, 'ctx_512': ctx_512, 'L0_attn_W_Q': _L0_attn_in['W_Q'], 'L0_attn_W_K': _L0_attn_in['W_K'], 'L0_attn_W_V': _L0_attn_in['W_V'], 'L0_attn_W_O': _L0_attn_in['W_O'], 'L0_xattn_Wq': _L0_xattn_in['Wq'], 'L0_xattn_Wkv_expand': _L0_xattn_in['Wkv_expand'], 'L0_xattn_Wout': _L0_xattn_in['Wout'], 'L0_ffn_U': _L0_ffn_in['U'], 'L0_ffn_V': _L0_ffn_in['V'], 'L0_ffn_W1': _L0_ffn_in['W1'], 'L0_ffn_b1': _L0_ffn_in['b1'], 'L0_ffn_W2': _L0_ffn_in['W2'], 'L0_ffn_b2': _L0_ffn_in['b2']}

def reference(x, ctx_512, L0_attn_W_Q, L0_attn_W_K, L0_attn_W_V, L0_attn_W_O, L0_xattn_Wq, L0_xattn_Wkv_expand, L0_xattn_Wout, L0_ffn_U, L0_ffn_V, L0_ffn_W1, L0_ffn_b1, L0_ffn_W2, L0_ffn_b2):
    import jax
    import jax.numpy as jnp

    def _L0_attn_ref(x, W_Q, W_K, W_V, W_O):
        import jax, jax.numpy as jnp
        import numpy as np
        import math
        D_MODEL = 256
        N_HEADS = 16
        D_HEAD = 128
        BATCH = 2
        SEQ = 256
        d_head = W_Q.shape[1]
        seq_len = x.shape[1]
        scale = 1.0 / math.sqrt(d_head)
        q = jnp.einsum('bsd,hed->bhse', x, W_Q)
        k = jnp.einsum('bsd,hed->bhse', x, W_K)
        v = jnp.einsum('bsd,hed->bhse', x, W_V)
        scores = jnp.einsum('bhse,bhme->bhsm', q, k) * scale
        causal = jnp.triu(jnp.ones((seq_len, seq_len), dtype=bool), k=1)
        scores = jnp.where(causal, jnp.float32(-1000000000.0), scores)
        pattern = jax.nn.softmax(scores, axis=-1)
        z = jnp.einsum('bhsm,bhme->bhse', pattern, v)
        out = jnp.einsum('bhse,hde->bsd', z, W_O)
        return out

    def _L0_xattn_ref(q, latent_kv, Wq, Wkv_expand, Wout):
        import jax, jax.numpy as jnp
        import numpy as np
        B, S, H, NH, L = (2, 256, 256, 16, 64)
        HD = H // NH
        b, sq, _ = q.shape
        sk = latent_kv.shape[1]
        qp = q @ Wq.T
        kv = latent_kv @ Wkv_expand.T
        k, v = jnp.split(kv, 2, axis=-1)
        qh = qp.reshape(b, sq, NH, HD).transpose(0, 2, 1, 3)
        kh = k.reshape(b, sk, NH, HD).transpose(0, 2, 1, 3)
        vh = v.reshape(b, sk, NH, HD).transpose(0, 2, 1, 3)
        inv_sqrt_d = 1.0 / jnp.sqrt(jnp.float32(HD))
        scores = jnp.einsum('bhqd,bhkd->bhqk', qh, kh) * inv_sqrt_d
        causal = jnp.tril(jnp.ones((sq, sk), dtype=bool))
        scores = jnp.where(causal, scores, jnp.finfo(scores.dtype).min)
        attn = jax.nn.softmax(scores, axis=-1)
        out = jnp.einsum('bhqk,bhkd->bhqd', attn, vh)
        out = out.transpose(0, 2, 1, 3).reshape(b, sq, H)
        return out @ Wout.T

    def _L0_ffn_ref(x, U, V, W1, b1, W2, b2):
        import jax, jax.numpy as jnp
        import numpy as np
        B, S, D, K, R = (4, 256, 256, 8, 64)
        h = jax.nn.relu(jnp.einsum('bsd,de->bse', x, W1) + b1)
        alpha = jax.nn.softmax(jnp.einsum('bse,ek->bsk', h, W2) + b2, axis=-1)
        vx = jnp.einsum('krd,bsd->bskr', V, x)
        uvx = jnp.einsum('kdr,bskr->bskd', U, vx)
        out = jnp.einsum('bsk,bskd->bsd', alpha, uvx)
        return out
    x = _layernorm(x + _L0_attn_ref(x, L0_attn_W_Q, L0_attn_W_K, L0_attn_W_V, L0_attn_W_O), axis=-1)
    x = _layernorm(x + _L0_xattn_ref(x, ctx_512, L0_xattn_Wq, L0_xattn_Wkv_expand, L0_xattn_Wout), axis=-1)
    x = _layernorm(x + _L0_ffn_ref(x, L0_ffn_U, L0_ffn_V, L0_ffn_W1, L0_ffn_b1, L0_ffn_W2, L0_ffn_b2), axis=-1)
    return x

_drawn_inputs = setup_inputs


def setup_inputs(seed=0):
    import zlib

    import numpy as np

    out = dict(_drawn_inputs(seed))
    spreads = {'L0_ffn_b1': (0.0, 0.8), 'L0_ffn_b2': (0.0, 0.8)}
    factors = {'L0_attn_W_Q': 7.803,
     'L0_attn_W_K': 7.643,
     'L0_xattn_Wq': 64.0,
     'L0_ffn_U': 3.126,
     'L0_ffn_V': 3.128,
     'L0_ffn_W1': 8.0,
     'L0_ffn_W2': 8.0}
    for name, (base, spread) in spreads.items():
        noise = np.random.default_rng([zlib.crc32(name.encode()), seed]).standard_normal(out[name].shape)
        drawn = base * np.exp(spread * noise) if base else spread * noise
        out[name] = jnp.asarray(drawn.astype(out[name].dtype))
    for name, factor in factors.items():
        out[name] = (out[name] * factor).astype(out[name].dtype)
    return out
```

```python
from contextlib import ExitStack

import concourse.bass as bass
from concourse import mybir

ALU = mybir.AluOpType
ACT = mybir.ActivationFunctionType
AX_X = mybir.AxisListType.X
F32 = mybir.dt.float32
F32R = mybir.dt.float32r
BF16 = mybir.dt.bfloat16

NB, S, D = 16, 56, 256
N = NB * S
P = 128
TILES = N // P
KD = D // P
NH, E = 16, 128
G = 4
NG = NH // G
SLOT = 64
ROWS = SLOT + S
PAIRS = NB // 2
HALF = N // 2
XH, XE, XL = 16, 16, 64
HG = 4
NHG = XH // HG
HP = XH // 2
EXPERTS, RANK = 8, 64
KR = EXPERTS * RANK // P
EPS = 1e-5
MASKED = -1e30
W = 4 * D
Q_, K_, V_, O_ = range(4)
ATTN_SCALE = float(E) ** -0.5
XATTN_SCALE = float(XE) ** -0.5


def build(nc, x, xT, weights, ctxT, wk_dup, wv, w2, b1, b2, out):
    with ExitStack() as ctx:
        def sb(name, shape, dt=F32):
            return ctx.enter_context(nc.sbuf_tensor(name, shape, dt))

        def ps(name, shape):
            return ctx.enter_context(nc.psum_tensor(name, shape, F32))

        def sem(name):
            return ctx.enter_context(nc.semaphore(name))

        raw = sb("raw", [P, 4, W])
        w_h = sb("w_h", [P, 4, W], F32R)
        w_l = sb("w_l", [P, 4, W], F32R)
        xraw = sb("xraw", [P, KD, NB, S])
        xt_h = sb("xt_h", [P, KD, NB, SLOT], F32R)
        xt_l = sb("xt_l", [P, KD, NB, SLOT], F32R)
        qT = sb("qT", [P, N])
        kT = sb("kT", [P, N])
        v = sb("v", [P, PAIRS, G * E])
        prob = sb("prob", [P, 8, SLOT])
        probn = sb("probn", [P, 8, SLOT])
        pT = sb("pT", [P, PAIRS, 2 * S])
        mx = sb("mx", [P, 8])
        rs = sb("rs", [P, 8])
        rinv = sb("rinv", [P, 8])
        z_h = sb("z_h", [P, G, N], F32R)
        z_l = sb("z_l", [P, G, N], F32R)
        acc = sb("acc", [P, TILES, D])
        ident = sb("ident", [P, P])
        ident_b = sb("ident_b", [P, P], BF16)
        mask = sb("mask", [P, 8, SLOT], BF16)
        hmask = sb("hmask", [P, HG])
        neg_half = sb("neg_half", [P, 2])
        ctx_s = sb("ctx_s", [XL, NB, 2, SLOT])
        wk_s = sb("wk_s", [XL, NHG, P])
        wv_s = sb("wv_s", [XL, D])
        k2 = sb("k2", [P, NHG, PAIRS, HG, S])
        v2 = sb("v2", [P, NB, HP, 2 * XE])

        w2_s = sb("w2_s", [P, KD, EXPERTS])
        b1_s = sb("b1_s", [P, KD])
        b2_s = sb("b2_s", [P, EXPERTS])
        stats = sb("stats", [P, TILES, 6])
        mv = sb("mv", [P, TILES, 2])
        veps = sb("veps", [P, TILES])
        rstd = sb("rstd", [P, TILES])
        mx2 = sb("mx2", [P, 2, XH])
        rs2 = sb("rs2", [P, 2, XH])
        rinv2 = sb("rinv2", [P, 2, XH])
        hT = sb("hT", [P, KD, 2 * P])
        lg = sb("lg", [P, 2, EXPERTS])
        lgm = sb("lgm", [P, 2])
        lgs = sb("lgs", [P, 2])
        lgr = sb("lgr", [P, 2])
        alpha = sb("alpha", [P, 2, EXPERTS])
        av = sb("av", [P, 2, EXPERTS * RANK])

        def flat(t):
            return t[:].rearrange({3: "p a b -> p (a b)", 4: "p a b c -> p (a b c)"}[len(t.shape)])

        def halves(t, at):
            return flat(t)[:, at:at + KD * N].rearrange("p (k n) -> p k n", k=KD)

        x1 = [halves(t, 0) for t in (xt_h, xt_l)]
        z2 = [halves(t, 0) for t in (z_h, z_l)]
        x2 = [halves(t, KD * N) for t in (z_h, z_l)]
        q2 = flat(v)[:, 0:NHG * PAIRS * ROWS].rearrange("p (h a n) -> p h a n", h=NHG, a=PAIRS)
        p2 = [raw[:, i, :].rearrange("p (h m) -> p h m", m=SLOT) for i in range(2)]
        pT2 = [raw[:, 2 + i, 0:HP * ROWS].rearrange("p (h n) -> p h n", h=HP) for i in range(2)]
        z2n = [prob[:, 4 * i:4 * i + 4, :].rearrange("p a m -> p (a m)") for i in range(2)]
        avT = [[flat(t)[:, i * 512:(i + 1) * 512].rearrange("p (c n) -> p c n", c=KR) for i in range(2)]
               for t in (xt_h, xt_l)]
        wq2 = [t[:, Q_, :].rearrange("p (k n) -> p k n", k=KD) for t in (w_h, w_l)]
        wout = [t[:, K_, :].rearrange("p (k n) -> p k n", k=KD)[:, :, 0:D] for t in (w_h, w_l)]
        w1 = [t[:, K_, :].rearrange("p (k n) -> p k n", k=KD)[:, :, D:2 * D] for t in (w_h, w_l)]
        vw = [t[:, V_, :].rearrange("p (k n) -> p k n", k=KD) for t in (w_h, w_l)]
        uw = [t[:, O_, :].rearrange("p (c n) -> p c n", c=KR) for t in (w_h, w_l)]

        b_qk = [ps(f"b_qk{i}", [P, 512]) for i in range(2)]
        b_st = ps("b_st", [P, 2, 512])
        b_s = b_st[:, 0, :]
        b_t = b_st[:, 1, :]
        b_z = ps("b_z", [P, 2, 512])
        b_vo = [ps(f"b_vo{i}", [P, 512]) for i in range(2)]

        d_xT, d_x, d_ctx, d_small = sem("d_xT"), sem("d_x"), sem("d_ctx"), sem("d_small")
        d_w = [sem(f"d_w{m}") for m in range(4)]
        zeroed, consts = sem("zeroed"), sem("consts")
        x_hi, x_lo = sem("x_hi"), sem("x_lo")
        w_hi = [sem(f"w_hi{m}") for m in range(4)]
        w_lo = [sem(f"w_lo{m}") for m in range(4)]
        qk_ready, qk_evac = sem("qk_ready"), sem("qk_evac")
        s_ready, max_done, sub_done = sem("s_ready"), sem("max_done"), sem("sub_done")
        exp_done, sum_done, recip_done, pn_ready = (
            sem("exp_done"), sem("sum_done"), sem("recip_done"), sem("pn_ready"))
        t_ready, pt_act, pt_dve = sem("t_ready"), sem("pt_act"), sem("pt_dve")
        z_ready, z_hi, z_lo = sem("z_ready"), sem("z_hi"), sem("z_lo")
        v_ready, v_evac = sem("v_ready"), sem("v_evac")
        o_ready, o_added = sem("o_ready"), sem("o_added")
        c_ready, c_act, c_dve = sem("c_ready"), sem("c_act"), sem("c_dve")
        bn_done, aggr_done, ve_ready, rstd_ready, ln_done = (
            sem("bn_done"), sem("aggr_done"), sem("ve_ready"), sem("rstd_ready"), sem("ln_done"))
        xT_ready, xT_hi, xT_lo = sem("xT_ready"), sem("xT_hi"), sem("xT_lo")
        q2_zeroed, p2_zeroed = sem("q2_zeroed"), sem("p2_zeroed")
        q2_ready, q2_act, q2_dve = sem("q2_ready"), sem("q2_act"), sem("q2_dve")
        s2_ready, max2_done, sub2_done, exp2_done, sum2_done, recip2_done = (
            sem("s2_ready"), sem("max2_done"), sem("sub2_done"), sem("exp2_done"), sem("sum2_done"),
            sem("recip2_done"))
        t2_ready, t2_evac, pv2_ready, z2_norm = sem("t2_ready"), sem("t2_evac"), sem("pv2_ready"), sem("z2_norm")
        z2_ready, z2_hi, z2_lo = sem("z2_ready"), sem("z2_hi"), sem("z2_lo")
        out2_ready, out2_added = sem("out2_ready"), sem("out2_added")
        h_ready, h_evac, lg_ready, lg_step, lg_exp, alpha_done = (
            sem("h_ready"), sem("h_evac"), sem("lg_ready"), sem("lg_step"), sem("lg_exp"), sem("alpha_done"))
        vx_ready, av_done, avT_ready, avT_hi, avT_lo = (
            sem("vx_ready"), sem("av_done"), sem("avT_ready"), sem("avT_hi"), sem("avT_lo"))
        u_ready, u_added, stored = sem("u_ready"), sem("u_added"), sem("stored")

        def qk_cols(m, i):
            return lambda t: t[:, m, :].rearrange("p (k n) -> p k n", k=KD)[:, :, i * E:(i + 1) * E]

        def ctx_uses(i):
            return (range(0), range(0, 5), range(5, 11), range(11, 16))[i]

        def out2_after(p):
            return {2: 0, 4: 1, 6: 2, 7: 3}.get(p)

        def o_tiles(j):
            return range(2 * j, min(2 * j + 2, TILES))

        block = ctx.enter_context(nc.Block())

        @block.sync
        def _(sp):
            sp.dma_start(xraw[:], xT.rearrange("(k p) b s -> p k b s", p=P)).then_inc(d_xT, 16)
            for m in (Q_, K_):
                sp.dma_start(raw[:, m, :], weights[0, m]).then_inc(d_w[m], 16)
            sp.dma_start(raw[:, V_, :], weights[0, V_]).then_inc(d_w[V_], 16)
            sp.dma_start(acc[:], x.rearrange("(t p) d -> p t d", p=P)).then_inc(d_x, 16)
            sp.dma_start(raw[:, O_, :], weights[0, O_]).then_inc(d_w[O_], 16)
            for r in range(2):
                sp.dma_start(ctx_s[:, :, r, 0:S], ctxT[:, :, 0:S]).then_inc(d_ctx, 16)
            sp.dma_start(wk_s[:], wk_dup).then_inc(d_ctx, 16)
            sp.dma_start(wv_s[:], wv).then_inc(d_ctx, 16)
            sp.dma_start(w2_s[:], w2).then_inc(d_small, 16)
            sp.dma_start(b1_s[:], b1).then_inc(d_small, 16)
            sp.dma_start(b2_s[:], b2.partition_broadcast(P)).then_inc(d_small, 16)
            with sp.Fori(1, NG + 1) as g:
                for m in range(4):
                    units = G if m in (Q_, K_) else 1
                    sp.wait_ge(w_hi[m], g * units)
                    sp.wait_ge(w_lo[m], g * units)
                    sp.dma_start(raw[:, m, :], weights[g, m]).then_inc(d_w[m], 16)
            for j in range(4):
                t = o_tiles(j)
                sp.wait_ge(ln_done, 8 + j + 1)
                sp.dma_start(out[t.start * P:t.stop * P].rearrange("(t p) d -> p t d", p=P),
                             acc[:, t.start:t.stop, :]).then_inc(stored, 16)
            sp.wait_ge(stored, 64)

        @block.gpsimd
        def _(pool):
            pool.memset(xt_h[:].bitcast(F32), 0.0).then_inc(zeroed, 1)
            pool.memset(xt_l[:].bitcast(F32), 0.0).then_inc(zeroed, 1)
            pool.memset(ident[:], 0.0).then_inc(consts, 1)
            pool.memset(mask[:], 0.0).then_inc(consts, 1)
            pool.memset(probn[:], 0.0).then_inc(consts, 1)
            pool.memset(pT[:], 0.0).then_inc(zeroed, 1)
            pool.wait_ge(consts, 3)
            pool.affine_select(out=ident[:], in_=ident[:], compare_op=ALU.not_equal, fill=1.0, base=0,
                               pattern=[[-1, P]], channel_multiplier=1).then_inc(consts, 1)
            for r in range(2):
                pool.wait_ge(consts, 4 + r)
                rows = mask[SLOT * r:SLOT * (r + 1)]
                pool.affine_select(out=rows, in_=rows, compare_op=ALU.is_ge, fill=MASKED, base=0,
                                   pattern=[[0, 8], [-1, SLOT]], channel_multiplier=1).then_inc(consts, 1)
            pool.wait_ge(consts, 6)
            pool.tensor_copy(ident_b[:], ident[:]).then_inc(consts, 1)

            pool.memset(neg_half[:], -0.5).then_inc(consts, 1)
            pool.memset(ctx_s[:, :, 0, S:SLOT], 0.0).then_inc(consts, 1)
            pool.memset(ctx_s[:, :, 1, S:SLOT], 0.0).then_inc(consts, 1)
            pool.memset(hmask[:], 1.0).then_inc(consts, 1)
            for r in range(2):
                rows = hmask[SLOT * r:SLOT * (r + 1)]
                pool.wait_ge(consts, 11 + 2 * r)
                pool.affine_select(out=rows, in_=rows, compare_op=ALU.is_ge, fill=0.0, base=0,
                                   pattern=[[-XE, HG]], channel_multiplier=1).then_inc(consts, 1)
                pool.wait_ge(consts, 12 + 2 * r)
                pool.affine_select(out=rows, in_=rows, compare_op=ALU.is_ge, fill=0.0, base=XE - 1,
                                   pattern=[[XE, HG]], channel_multiplier=-1).then_inc(consts, 1)
            pool.wait_ge(consts, 15)
            pool.memset(v2[:], 0.0).then_inc(consts, 1)

            def norm(s, first=False):
                pool.wait_ge(recip_done, s + 1)
                if not first:
                    pool.wait_ge(t_ready, s)
                pool.tensor_tensor(probn[0:ROWS, :, 0:S], prob[0:ROWS, :, 0:S],
                                   rinv[0:ROWS, :].unsqueeze(2).broadcast_to([ROWS, 8, S]),
                                   ALU.mult).then_inc(pn_ready, 1)

            def split_lo(m, cols, count):
                pool.wait_ge(w_hi[m], count)
                pool.tensor_tensor(cols(w_l), cols(raw), cols(w_h).bitcast(F32), ALU.subtract).then_inc(w_lo[m], 1)

            def group(g, first=False):
                for i in range(G):
                    s = g * G + i
                    norm(s, first and i == 0)
                    for m in (Q_, K_):
                        pool.wait_ge(qk_ready, s * 4 + 4)
                        split_lo(m, qk_cols(m, i), (g + 1) * G + i + 1)
                    if i == 1:
                        pool.wait_ge(v_ready, (g + 1) * PAIRS)
                        split_lo(V_, lambda t: t[:, V_, :], g + 2)
                    if i == 3:
                        if not first:
                            pool.wait_ge(o_ready, g * 4)
                        split_lo(O_, lambda t: t[:, O_, :], g + 1)

            group(0, first=True)
            with pool.Fori(1, NG) as g:
                group(g)
            pool.wait_ge(z_ready, 2 * NH)
            pool.memset(q2, 0.0).then_inc(q2_zeroed, 1)
            for m in (Q_, K_):
                pool.wait_ge(w_lo[m], (NG + 1) * G)
            pool.memset(raw[:, 0:2, :], 0.0).then_inc(p2_zeroed, 1)
            pool.wait_ge(o_ready, NG * 4)
            split_lo(O_, lambda t: t[:, O_, :], NG + 1)
            for n in range(12):
                t = o_tiles(n % 4)
                pool.wait_ge(ve_ready, n + 1)
                pool.tensor_tensor(rstd[:, t.start:t.stop], veps[:, t.start:t.stop], neg_half[:, 0:len(t)],
                                   ALU.pow).then_inc(rstd_ready, 1)

        @block.scalar
        def _(act):
            def split_hi(m, cols, arrived):
                act.wait_ge(d_w[m], arrived * 16)
                act.copy(cols(w_h), cols(raw)).then_inc(w_hi[m], 1)

            act.wait_ge(d_xT, 16)
            act.wait_ge(zeroed, 2)
            for k in range(KD):
                act.copy(xt_h[:, k, :, 0:S], xraw[:, k]).then_inc(x_hi, 1)
            for m in (Q_, K_):
                split_hi(m, qk_cols(m, 0), 1)

            def evac_qk(s, first=False):
                if not first:
                    act.wait_ge(s_ready, s)
                for n in range(4):
                    act.wait_ge(qk_ready, s * 4 + n + 1)
                    dst = (qT, kT)[n // 2]
                    act.copy(dst[:, (n % 2) * HALF:(n % 2 + 1) * HALF],
                             b_qk[n % 2][:, 0:HALF]).then_inc(qk_evac, 1)

            def evac_pT(s):
                act.wait_ge(t_ready, s + 1)
                act.copy(pT[0:S, :, 0:S],
                         b_t[0:S, :].rearrange("p (a m) -> p a m", m=SLOT)[:, :, 0:S]).then_inc(pt_act, 1)

            def exp(s):
                act.wait_ge(sub_done, s + 1)
                act.activation(prob[0:ROWS, :, 0:S], prob[0:ROWS, :, 0:S], ACT.Exp,
                               scale=ATTN_SCALE).then_inc(exp_done, 1)

            def evac_z_hi(s, i):
                for c in range(2):
                    act.wait_ge(z_ready, s * 2 + c + 1)
                    act.copy(z_h[:, i, c * HALF:(c + 1) * HALF], b_z[:, c, 0:HALF]).then_inc(z_hi, 1)

            def evac_ctx(n):
                act.wait_ge(c_ready, n + 1)
                if n < 8:
                    hg, c = n % 4, n // 4
                    src = b_vo[n % 2][0:SLOT, 0:HALF].rearrange("p (a r m) -> p a r m", r=2, m=S)[:, :, 0, :]
                    for h in range(HG):
                        ins = act.activation(k2[0:SLOT, hg, 4 * c:4 * c + 4, h, :], src, ACT.Copy,
                                             scale=hmask[0:SLOT, h:h + 1])
                else:
                    b = 2 * (n - 8)
                    src = b_vo[n % 2][0:S, :].rearrange("p (b h r e) -> p b h r e", b=2, h=HP, r=2)[:, :, :, 0, :]
                    ins = act.copy(v2[0:S, b:b + 2, :, 0:XE], src)
                ins.then_inc(c_act, 1)

            def group(g, first=False):
                for i in range(G):
                    s = g * G + i
                    begin = first and i == 0
                    evac_qk(s, begin)
                    if begin:
                        for h in range(1, G):
                            for m in (Q_, K_):
                                split_hi(m, qk_cols(m, h), 1)
                        split_hi(V_, lambda t: t[:, V_, :], 1)
                    else:
                        evac_pT(s - 1)
                    exp(s)
                    if not begin:
                        evac_z_hi(s - 1, (i - 1) % G)
                    if i == 0:
                        for j in range(PAIRS):
                            act.wait_ge(v_ready, g * PAIRS + j + 1)
                            act.copy(v[0:ROWS, j, :], b_vo[j % 2][0:ROWS, :]).then_inc(v_evac, 1)
                    if first and i > 0:
                        if i == 1:
                            act.wait_ge(consts, 16)
                        for n in ctx_uses(i):
                            evac_ctx(n)
                    for m in (Q_, K_):
                        split_hi(m, qk_cols(m, i), g + 2)
                    if i == 1:
                        split_hi(V_, lambda t: t[:, V_, :], g + 2)
                    if i == 3:
                        if not first:
                            act.wait_ge(o_ready, g * 4)
                        split_hi(O_, lambda t: t[:, O_, :], g + 1)

            group(0, first=True)
            with act.Fori(1, NG) as g:
                group(g)
            evac_pT(NH - 1)
            evac_z_hi(NH - 1, G - 1)
            act.wait_ge(o_ready, NG * 4)
            split_hi(O_, lambda t: t[:, O_, :], NG + 1)

            def evac_xT(n, dst):
                t = o_tiles(n % 4)
                act.wait_ge(xT_ready, n + 1)
                act.copy(dst[0][:, :, t.start * P:t.stop * P],
                         b_st[:, n % 2 if n < 4 else 0, :].rearrange("p (k n) -> p k n", k=KD)[:, :, 0:len(t) * P]).then_inc(xT_hi, 1)

            for j in range(4):
                evac_xT(j, x1)
            act.wait_ge(q2_zeroed, 1)
            for n in range(8):
                hg, c = n % 4, n // 4
                act.wait_ge(q2_ready, n + 1)
                act.copy(q2[0:SLOT, hg, 4 * c:4 * c + 4, 0:S],
                         b_qk[n % 2][0:SLOT, 0:HALF].rearrange("p (a r m) -> p a r m", r=2, m=S)[:, :, 0, :]
                         ).then_inc(q2_act, 1)
            for u in range(PAIRS + 3):
                if u < PAIRS:
                    act.wait_ge(sub2_done, u + 1)
                    act.activation(p2[u % 2][0:ROWS, :, 0:S], p2[u % 2][0:ROWS, :, 0:S], ACT.Exp,
                                   scale=XATTN_SCALE).then_inc(exp2_done, 1)
                if 0 <= u - 1 < PAIRS:
                    p = u - 1
                    act.wait_ge(t2_ready, p + 1)
                    if p >= 2:
                        act.wait_ge(pv2_ready, p - 1)
                    act.copy(pT2[p % 2][0:ROWS, :, :],
                             b_st[0:ROWS, :, :].rearrange("p a (h n) -> p (a h) n", n=P)[:, :, 0:ROWS]
                             ).then_inc(t2_evac, 1)
                if 0 <= u - 3 < PAIRS:
                    p = u - 3
                    act.wait_ge(z2_ready, p + 1)
                    for k in range(KD):
                        ins = act.copy(z2[0][:, k, p * 2 * S:(p + 1) * 2 * S].rearrange("p (r m) -> p r m", r=2),
                                       b_qk[0][:, k * D:k * D + P].rearrange("p (r m) -> p r m", r=2)[:, :, 0:S])
                    ins.then_inc(z2_hi, 1)
            act.wait_ge(d_small, 48)
            for j in range(5):
                if j < 4:
                    evac_xT(4 + j, x2)
                if j > 0:
                    for n, t in enumerate(o_tiles(j - 1)):
                        act.wait_ge(avT_ready, t + 1)
                        act.copy(avT[0][n], (b_z[:, 1, :], b_qk[0][:])[n].rearrange("p (c n) -> p c n", c=KR)
                                 ).then_inc(avT_hi, 1)
                if j < 4:
                    cols = len(o_tiles(j)) * P
                    act.wait_ge(h_ready, j + 1)
                    for m in range(KD):
                        ins = act.activation(hT[:, m, 0:cols], b_st[:, 1, m * D:m * D + cols], ACT.Relu,
                                             bias=b1_s[:, m:m + 1])
                    ins.then_inc(h_evac, 1)
                    act.wait_ge(lg_step, 3 * j + 3)
                    act.activation(lg[:, 0:len(o_tiles(j)), :], lg[:, 0:len(o_tiles(j)), :], ACT.Exp).then_inc(lg_exp, 1)

        @block.vector
        def _(dve):
            def split_lo(m, cols):
                dve.wait_ge(w_hi[m], 1)
                dve.tensor_tensor(cols(w_l), cols(raw), cols(w_h).bitcast(F32), ALU.subtract).then_inc(w_lo[m], 1)

            dve.wait_ge(zeroed, 2)
            for k in range(KD):
                dve.wait_ge(x_hi, k + 1)
                dve.tensor_tensor(xt_l[:, k, :, 0:S], xraw[:, k], xt_h[:, k, :, 0:S].bitcast(F32),
                                  ALU.subtract).then_inc(x_lo, 1)
            for h in range(G):
                for m in (Q_, K_):
                    dve.wait_ge(w_hi[m], h + 1)
                    split_lo(m, qk_cols(m, h))
            split_lo(V_, lambda t: t[:, V_, :])

            def evac_pT(s):
                dve.wait_ge(t_ready, s + 1)
                dve.tensor_copy(pT[SLOT:ROWS, :, S:2 * S],
                                b_t[SLOT:ROWS, :].rearrange("p (a m) -> p a m", m=SLOT)[:, :, 0:S]).then_inc(pt_dve, 1)

            def center(s, first=False):
                dve.wait_ge(s_ready, s + 1)
                scores = b_s[0:ROWS, :].rearrange("p (a m) -> p a m", m=SLOT)[:, :, 0:S]
                dve.tensor_reduce(mx[0:ROWS, :], scores, AX_X, ALU.max).then_inc(max_done, 1)
                dve.wait_ge(max_done, s + 1)
                if not first:
                    dve.wait_ge(pn_ready, s)
                dve.tensor_tensor(prob[0:ROWS, :, 0:S], scores,
                                  mx[0:ROWS, :].unsqueeze(2).broadcast_to([ROWS, 8, S]),
                                  ALU.subtract).then_inc(sub_done, 1)

            def row_sums(s):
                dve.wait_ge(exp_done, s + 1)
                dve.tensor_reduce(rs[0:ROWS, :], prob[0:ROWS, :, 0:S], AX_X, ALU.add).then_inc(sum_done, 1)
                dve.wait_ge(sum_done, s + 1)
                dve.reciprocal(rinv[0:ROWS, :], rs[0:ROWS, :]).then_inc(recip_done, 1)

            def evac_z_lo(s, i):
                for c in range(2):
                    dve.wait_ge(z_hi, s * 2 + c + 1)
                    cols = slice(c * HALF, (c + 1) * HALF)
                    dve.tensor_tensor(z_l[:, i, cols], b_z[:, c, 0:HALF], z_h[:, i, cols].bitcast(F32),
                                      ALU.subtract).then_inc(z_lo, 1)

            def add_o_step(g, j):
                dve.wait_ge(o_ready, g * 4 + j + 1)
                t = o_tiles(j)
                a = acc[:, t.start:t.stop, :]
                dve.tensor_tensor(a, b_vo[j % 2][:, 0:len(t) * D].rearrange("p (t d) -> p t d", d=D), a,
                                  ALU.add).then_inc(o_added, 1)

            def add_o(g):
                for j in range(4):
                    add_o_step(g, j)

            def evac_ctx(n):
                dve.wait_ge(c_ready, n + 1)
                if n < 8:
                    hg, c = n % 4, n // 4
                    src = b_vo[n % 2][SLOT:P, 0:HALF].rearrange("p (a r m) -> p a r m", r=2, m=S)[:, :, 1, :]
                    for h in range(HG):
                        ins = dve.tensor_scalar(k2[SLOT:P, hg, 4 * c:4 * c + 4, h, :], src,
                                                hmask[SLOT:P, h:h + 1], None, ALU.mult)
                else:
                    b = 2 * (n - 8)
                    src = b_vo[n % 2][SLOT:ROWS, :].rearrange("p (b h r e) -> p b h r e", b=2, h=HP, r=2)[:, :, :, 1, :]
                    ins = dve.tensor_copy(v2[SLOT:ROWS, b:b + 2, :, XE:2 * XE], src)
                ins.then_inc(c_dve, 1)

            def group(g, first=False):
                for i in range(G):
                    s = g * G + i
                    begin = first and i == 0
                    if not begin:
                        evac_pT(s - 1)
                    center(s, begin)
                    row_sums(s)
                    if not begin:
                        evac_z_lo(s - 1, (i - 1) % G)
                    if first and i > 0:
                        if i == 1:
                            dve.wait_ge(consts, 16)
                        for n in ctx_uses(i):
                            evac_ctx(n)
                    if i == 0 and not first:
                        add_o(g - 1)

            dve.wait_ge(zeroed, 3)
            dve.wait_ge(d_x, 16)
            group(0, first=True)
            with dve.Fori(1, NG) as g:
                group(g)
            evac_pT(NH - 1)
            evac_z_lo(NH - 1, G - 1)

            def moments(layer, j, added):
                sem_, count = added
                tiles = o_tiles(j)
                dve.wait_ge(sem_, count)
                for t in tiles:
                    dve.bn_stats(stats[:, t, :], acc[:, t, :]).then_inc(bn_done, 1)
                for t in tiles:
                    dve.wait_ge(bn_done, layer * TILES + t + 1)
                    dve.bn_aggr(mv[:, t, :], stats[:, t, :]).then_inc(aggr_done, 1)
                dve.wait_ge(aggr_done, layer * TILES + tiles.stop)
                dve.tensor_scalar(veps[:, tiles.start:tiles.stop], mv[:, tiles.start:tiles.stop, 1], EPS, None,
                                  ALU.add).then_inc(ve_ready, 1)

            def normalize(layer, j):
                dve.wait_ge(rstd_ready, layer * 4 + j + 1)
                for t in o_tiles(j):
                    ins = dve.tensor_scalar(acc[:, t, :], acc[:, t, :], mv[:, t, 0:1], rstd[:, t:t + 1],
                                            ALU.subtract, ALU.mult)
                ins.then_inc(ln_done, 1)

            def evac_xT(n, dst):
                t = o_tiles(n % 4)
                cols = slice(t.start * P, t.stop * P)
                dve.wait_ge(xT_hi, n + 1)
                dve.tensor_tensor(dst[1][:, :, cols],
                                  b_st[:, n % 2 if n < 4 else 0, :].rearrange("p (k n) -> p k n", k=KD)[:, :, 0:len(t) * P],
                                  dst[0][:, :, cols].bitcast(F32), ALU.subtract).then_inc(xT_lo, 1)

            for j in range(6):
                if j < 4:
                    if j == 0:
                        dve.wait_ge(o_added, NG * 4 - 4)
                    add_o_step(NG - 1, j)
                    moments(0, j, (o_added, NG * 4 - 4 + j + 1))
                if 0 <= j - 1 < 4:
                    normalize(0, j - 1)
                if 0 <= j - 2 < 4:
                    evac_xT(j - 2, x1)
            dve.wait_ge(q2_zeroed, 1)
            for n in range(8):
                hg, c = n % 4, n // 4
                dve.wait_ge(q2_ready, n + 1)
                dve.tensor_copy(q2[SLOT:P, hg, 4 * c:4 * c + 4, SLOT:ROWS],
                                b_qk[n % 2][SLOT:P, 0:HALF].rearrange("p (a r m) -> p a r m", r=2, m=S)[:, :, 1, :]
                                ).then_inc(q2_dve, 1)
            dve.wait_ge(p2_zeroed, 1)
            dve.wait_ge(pn_ready, NH)
            for u in range(PAIRS + 4):
                if u < PAIRS:
                    sc = b_z[0:ROWS, :, :].rearrange("p a (h m) -> p (a h) m", m=SLOT)[:, :, 0:S]
                    m_ = mx2[0:ROWS, u % 2, :]
                    dve.wait_ge(s2_ready, u + 1)
                    dve.tensor_reduce(m_, sc, AX_X, ALU.max).then_inc(max2_done, 1)
                    dve.wait_ge(max2_done, u + 1)
                    if u >= 2:
                        dve.wait_ge(t2_ready, u - 1)
                    dve.tensor_tensor(p2[u % 2][0:ROWS, :, 0:S], sc,
                                      m_.unsqueeze(2).broadcast_to([ROWS, XH, S]), ALU.subtract).then_inc(sub2_done, 1)
                if 0 <= u - 2 < PAIRS:
                    p = u - 2
                    dve.wait_ge(pv2_ready, p + 1)
                    dve.wait_ge(recip2_done, p + 1)
                    if p >= 2:
                        dve.wait_ge(z2_ready, p - 1)
                    dve.tensor_tensor(z2n[p % 2][0:ROWS, :].rearrange("p (h e) -> p h e", e=XE),
                                      b_vo[p % 2][0:ROWS, 0:D].rearrange("p (h e) -> p h e", e=XE),
                                      rinv2[0:ROWS, p % 2, :].unsqueeze(2).broadcast_to([ROWS, XH, XE]),
                                      ALU.mult).then_inc(z2_norm, 1)
                if 0 <= u - 3 < PAIRS:
                    p = u - 3
                    dve.wait_ge(z2_hi, p + 1)
                    for k in range(KD):
                        cols = slice(p * 2 * S, (p + 1) * 2 * S)
                        ins = dve.tensor_tensor(
                            z2[1][:, k, cols].rearrange("p (r m) -> p r m", r=2),
                            b_qk[0][:, k * D:k * D + P].rearrange("p (r m) -> p r m", r=2)[:, :, 0:S],
                            z2[0][:, k, cols].rearrange("p (r m) -> p r m", r=2).bitcast(F32), ALU.subtract)
                    ins.then_inc(z2_lo, 1)
                if u < PAIRS:
                    dve.wait_ge(exp2_done, u + 1)
                    dve.tensor_reduce(rs2[0:ROWS, u % 2, :], p2[u % 2][0:ROWS, :, 0:S], AX_X,
                                      ALU.add).then_inc(sum2_done, 1)
                    dve.wait_ge(sum2_done, u + 1)
                    dve.reciprocal(rinv2[0:ROWS, u % 2, :], rs2[0:ROWS, u % 2, :]).then_inc(recip2_done, 1)
                if 0 <= u - 4 and (j := out2_after(u - 4)) is not None:
                    t = o_tiles(j)
                    a = acc[:, t.start:t.stop, :]
                    dve.wait_ge(out2_ready, j + 1)
                    dve.wait_ge(xT_ready, j + 1)
                    dve.tensor_tensor(a, b_qk[1][:, 0:len(t) * D].rearrange("p (t d) -> p t d", d=D), a,
                                      ALU.add).then_inc(out2_added, 1)
                    moments(1, j, (out2_added, j + 1))
                    if j > 0:
                        normalize(1, j - 1)
            normalize(1, 3)
            dve.wait_ge(d_small, 48)
            for j in range(5):
                if j < 4:
                    evac_xT(4 + j, x2)
                if j > 0:
                    for n, t in enumerate(o_tiles(j - 1)):
                        dve.wait_ge(avT_hi, t + 1)
                        dve.tensor_tensor(avT[1][n], (b_z[:, 1, :], b_qk[0][:])[n].rearrange("p (c n) -> p c n", c=KR),
                                          avT[0][n].bitcast(F32), ALU.subtract).then_inc(avT_lo, 1)
                if j < 4:
                    tiles = o_tiles(j)
                    nt = len(tiles)
                    dve.wait_ge(lg_ready, j + 1)
                    dve.tensor_tensor(lg[:, 0:nt, :], b_z[:, 0, 0:nt * EXPERTS].rearrange("p (t e) -> p t e", e=EXPERTS),
                                      b2_s[:].unsqueeze(1).broadcast_to([P, nt, EXPERTS]), ALU.add).then_inc(lg_step, 1)
                    dve.wait_ge(lg_step, 3 * j + 1)
                    dve.tensor_reduce(lgm[:, 0:nt], lg[:, 0:nt, :], AX_X, ALU.max).then_inc(lg_step, 1)
                    dve.wait_ge(lg_step, 3 * j + 2)
                    dve.tensor_tensor(lg[:, 0:nt, :], lg[:, 0:nt, :],
                                      lgm[:, 0:nt].unsqueeze(2).broadcast_to([P, nt, EXPERTS]),
                                      ALU.subtract).then_inc(lg_step, 1)
                    dve.wait_ge(lg_exp, j + 1)
                    dve.tensor_reduce(lgs[:, 0:nt], lg[:, 0:nt, :], AX_X, ALU.add).then_inc(alpha_done, 1)
                    dve.wait_ge(alpha_done, 3 * j + 1)
                    dve.reciprocal(lgr[:, 0:nt], lgs[:, 0:nt]).then_inc(alpha_done, 1)
                    dve.wait_ge(alpha_done, 3 * j + 2)
                    dve.tensor_tensor(alpha[:, 0:nt, :], lg[:, 0:nt, :],
                                      lgr[:, 0:nt].unsqueeze(2).broadcast_to([P, nt, EXPERTS]),
                                      ALU.mult).then_inc(alpha_done, 1)
                    dve.wait_ge(alpha_done, 3 * j + 3)
                    for n, t in enumerate(tiles):
                        dve.wait_ge(vx_ready, t + 1)
                        dve.tensor_tensor(av[:, n, :].rearrange("p (e r) -> p e r", r=RANK),
                                          b_vo[n][:].rearrange("p (e r) -> p e r", r=RANK),
                                          alpha[:, n, :].unsqueeze(2).broadcast_to([P, EXPERTS, RANK]),
                                          ALU.mult).then_inc(av_done, 1)
                if j > 0:
                    t = o_tiles(j - 1)
                    a = acc[:, t.start:t.stop, :]
                    dve.wait_ge(u_ready, j)
                    dve.tensor_tensor(a, b_qk[1][:, 0:len(t) * D].rearrange("p (t d) -> p t d", d=D), a,
                                      ALU.add).then_inc(u_added, 1)
                    moments(2, j - 1, (u_added, j))
                    normalize(2, j - 1)

        @block.tensor
        def _(pe):
            def three(out_, terms, **kw):
                last = None
                steps = [(a, b) for (ah, al), (bh, bl) in terms for a, b in ((ah, bh), (al, bh), (ah, bl))]
                for n, (a, b) in enumerate(steps):
                    last = pe.matmul(out_, a, b, start=(n == 0), stop=(n == len(steps) - 1), **kw)
                return last

            def qk(s, i, first=False):
                for m in (Q_, K_):
                    pe.wait_ge(w_hi[m], s + 1)
                    pe.wait_ge(w_lo[m], s + 1)
                    wh, wl = (qk_cols(m, i)(t) for t in (w_h, w_l))
                    for c in range(2):
                        if not first or m == K_:
                            pe.wait_ge(qk_evac, s * 4 + 2 * m + c - 1)
                        batches = slice(c * NB // 2, (c + 1) * NB // 2)
                        three(b_qk[c][:, 0:HALF],
                              [((wh[:, k, :], wl[:, k, :]),
                                (xt_h[:, k, batches, 0:S], xt_l[:, k, batches, 0:S])) for k in range(KD)]
                              ).then_inc(qk_ready, 1)

            def transposes(s):
                pe.wait_ge(pn_ready, s + 1)
                for t in range(4):
                    mm = pe.transpose(b_t[0:ROWS, t * P:t * P + ROWS],
                                      probn[0:ROWS, 2 * t:2 * t + 2, :].rearrange("p a m -> p (a m)")[:, 0:ROWS],
                                      ident[0:ROWS, 0:ROWS])
                mm.then_inc(t_ready, 1)

            def scores(s, first=False):
                pe.wait_ge(qk_evac, s * 4 + 4)
                if not first:
                    pe.wait_ge(sub_done, s)
                pe.matmul(b_s, ident_b[:], mask[:].rearrange("p a m -> p (a m)"), start=True, stop=False,
                          skip_group_check=True)
                for b in range(NB):
                    t, r, c = b // 4, b // 2 % 2, b % 2
                    cols = slice(b * S, (b + 1) * S)
                    mm = pe.matmul(b_s[SLOT * r:SLOT * r + S, t * P + SLOT * c:t * P + SLOT * c + S],
                                   qT[:, cols], kT[:, cols], start=False, stop=True, skip_group_check=True)
                mm.then_inc(s_ready, 1)

            def pv(s, i, g, first=False):
                pe.wait_ge(pt_act, s + 1)
                pe.wait_ge(pt_dve, s + 1)
                pe.wait_ge(v_evac, (g + 1) * PAIRS)
                for c in range(2):
                    if not first:
                        pe.wait_ge(z_hi, s * 2 + c - 1)
                        pe.wait_ge(z_lo, s * 2 + c - 1)
                    for p in range(4):
                        pair = 4 * c + p
                        mm = pe.matmul(b_z[:, c, p * 2 * S:(p + 1) * 2 * S], v[0:ROWS, pair, i * E:(i + 1) * E],
                                       pT[0:ROWS, pair, :], start=True, stop=True)
                    mm.then_inc(z_ready, 1)

            def values(g):
                pe.wait_ge(w_hi[V_], g + 1)
                pe.wait_ge(w_lo[V_], g + 1)
                wh, wl = (t[:, V_, :].rearrange("p (k n) -> p k n", k=KD) for t in (w_h, w_l))
                for j in range(PAIRS):
                    if j >= 2:
                        pe.wait_ge(v_evac, g * PAIRS + j - 1)
                    xs = [tuple(t[:, k, 2 * j:2 * j + 2, :].rearrange("p b s -> p (b s)")[:, 0:ROWS]
                                for t in (xt_h, xt_l)) for k in range(KD)]
                    three(b_vo[j % 2][0:ROWS, :],
                          [(xs[k], (wh[:, k, :], wl[:, k, :])) for k in range(KD)]).then_inc(v_ready, 1)

            def project(g, after_values=True):
                pe.wait_ge(w_hi[O_], g + 1)
                pe.wait_ge(w_lo[O_], g + 1)
                pe.wait_ge(z_hi, (g + 1) * G * 2)
                pe.wait_ge(z_lo, (g + 1) * G * 2)
                wh, wl = (t[:, O_, :].rearrange("p (h n) -> p h n", h=G) for t in (w_h, w_l))
                for j in range(4):
                    if j < 2 and after_values:
                        pe.wait_ge(v_evac, (g + 1) * PAIRS + PAIRS - 1 + j)
                    else:
                        pe.wait_ge(o_added, g * 4 + j - 1)
                    for n, t in enumerate(o_tiles(j)):
                        cols = slice(t * P, (t + 1) * P)
                        mm = three(b_vo[j % 2][:, n * D:(n + 1) * D],
                                   [((z_h[:, h, cols], z_l[:, h, cols]), (wh[:, h, :], wl[:, h, :]))
                                    for h in range(G)])
                    mm.then_inc(o_ready, 1)

            pe.wait_ge(x_hi, KD)
            pe.wait_ge(x_lo, KD)
            pe.wait_ge(consts, 7)

            def group(g, first=False):
                for i in range(G):
                    s = g * G + i
                    begin = first and i == 0
                    qk(s, i, begin)
                    if not begin:
                        transposes(s - 1)
                    scores(s, begin)
                    if i == 0:
                        if not first:
                            pv(s - 1, G - 1, g - 1)
                        values(g)
                        if not first:
                            project(g - 1)
                    else:
                        pv(s - 1, i - 1, g, first and i == 1)
                        if first:
                            if i == 1:
                                pe.wait_ge(d_ctx, 64)
                                pe.wait_ge(consts, 10)
                            for n in ctx_uses(i):
                                latent(n)

            def latent(n):
                if n < 2:
                    pe.wait_ge(v_evac, PAIRS)
                else:
                    pe.wait_ge(c_act, n - 1)
                    pe.wait_ge(c_dve, n - 1)
                if n < 8:
                    hg, c = n % 4, n // 4
                    mm = pe.matmul(b_vo[n % 2][:, 0:HALF], wk_s[:, hg, :], ctx_s[:, 8 * c:8 * c + 8, 0, 0:S],
                                   start=True, stop=True)
                else:
                    for i in range(2):
                        b = 2 * (n - 8) + i
                        mm = pe.matmul(b_vo[n % 2][0:ROWS, i * D:(i + 1) * D],
                                       ctx_s[:, b, :, :].rearrange("p r m -> p (r m)")[:, 0:ROWS], wv_s[:],
                                       start=True, stop=True)
                mm.then_inc(c_ready, 1)

            group(0, first=True)
            pe.wait_ge(c_act, 16)
            pe.wait_ge(c_dve, 16)
            with pe.Fori(1, NG) as g:
                group(g)
            transposes(NH - 1)
            pv(NH - 1, G - 1, NG - 1)
            project(NG - 1, after_values=False)

            def transpose_x(n):
                pe.wait_ge(ln_done, n + 1)
                if n in (2, 3):
                    pe.wait_ge(xT_lo, n - 1)
                elif n > 4:
                    pe.wait_ge(xT_lo, n)
                for i, t in enumerate(o_tiles(n % 4)):
                    for k in range(KD):
                        mm = pe.transpose(b_st[:, n % 2 if n < 4 else 0, k * D + i * P:k * D + (i + 1) * P],
                                          acc[:, t, k * P:(k + 1) * P], ident[:])
                mm.then_inc(xT_ready, 1)

            def queries(n):
                hg, c = n % 4, n // 4
                pe.wait_ge(xT_lo, 2 * c + 2)
                if n >= 2:
                    pe.wait_ge(q2_act, n - 1)
                    pe.wait_ge(q2_dve, n - 1)
                cols = slice(c * HALF, (c + 1) * HALF)
                three(b_qk[n % 2][:, 0:HALF],
                      [(tuple(w[:, k, hg * P:(hg + 1) * P] for w in wq2), tuple(x[:, k, cols] for x in x1))
                       for k in range(KD)]).then_inc(q2_ready, 1)

            pe.wait_ge(w_lo[Q_], (NG + 1) * G)
            for j in range(4):
                transpose_x(j)
                if j == 2:
                    queries(0)
                    queries(1)
            for n in range(2, 8):
                queries(n)

            def scores2(p):
                pe.wait_ge(q2_act, 4 * (p // 4) + 4)
                pe.wait_ge(q2_dve, 4 * (p // 4) + 4)
                if p > 0:
                    pe.wait_ge(sub2_done, p)
                for half in range(2):
                    pe.matmul(b_z[:, half, :], ident_b[:], mask[:].rearrange("p a m -> p (a m)"), start=True,
                              stop=False, skip_group_check=True)
                    for i in range(2):
                        hg = 2 * half + i
                        mm = pe.matmul(b_z[0:ROWS, half, i * D:(i + 1) * D].rearrange("p (h m) -> p h m", m=SLOT)[:, :, 0:S],
                                       q2[:, hg, p, :], k2[:, hg, p, :, :], start=False, stop=True,
                                       skip_group_check=True)
                mm.then_inc(s2_ready, 1)

            def transposes2(p):
                pe.wait_ge(exp2_done, p + 1)
                if p > 0:
                    pe.wait_ge(t2_evac, p)
                for h in range(HP):
                    mm = pe.transpose(b_st[0:ROWS, h // 4, (h % 4) * P:(h % 4) * P + ROWS],
                                      p2[p % 2][0:ROWS, 2 * h:2 * h + 2, :].rearrange("p a m -> p (a m)")[:, 0:ROWS],
                                      ident[0:ROWS, 0:ROWS])
                mm.then_inc(t2_ready, 1)

            def pv2(p):
                pe.wait_ge(t2_evac, p + 1)
                if p >= 2:
                    pe.wait_ge(z2_norm, p - 1)
                for r in range(2):
                    for h in range(HP):
                        mm = pe.matmul(b_vo[p % 2][SLOT * r:SLOT * r + S, h * 2 * XE:(h + 1) * 2 * XE],
                                       pT2[p % 2][0:ROWS, h, SLOT * r:SLOT * r + S], v2[0:ROWS, 2 * p + r, h, :],
                                       start=True, stop=True)
                mm.then_inc(pv2_ready, 1)

            def transposes3(p):
                pe.wait_ge(z2_norm, p + 1)
                if p > 0:
                    pe.wait_ge(z2_lo, p)
                for k in range(KD):
                    mm = pe.transpose(b_qk[0][:, k * D:k * D + ROWS], z2n[p % 2][0:ROWS, k * P:(k + 1) * P],
                                      ident[0:ROWS, 0:ROWS])
                mm.then_inc(z2_ready, 1)

            def out2(p, j):
                pe.wait_ge(z2_lo, p + 1)
                if j > 0:
                    pe.wait_ge(out2_added, j)
                for i, t in enumerate(o_tiles(j)):
                    cols = slice(t * P, (t + 1) * P)
                    mm = three(b_qk[1][:, i * D:(i + 1) * D],
                               [(tuple(z[:, k, cols] for z in z2), tuple(w[:, k, :] for w in wout))
                                for k in range(KD)])
                mm.then_inc(out2_ready, 1)

            pe.wait_ge(w_lo[K_], (NG + 1) * G)
            pe.wait_ge(w_lo[O_], NG + 1)
            for u in range(PAIRS + 4):
                if u < PAIRS:
                    scores2(u)
                if 0 <= u - 1 < PAIRS:
                    transposes2(u - 1)
                if 0 <= u - 2 < PAIRS:
                    pv2(u - 2)
                if 0 <= u - 3 < PAIRS:
                    transposes3(u - 3)
                if 0 <= u - 4 and (j := out2_after(u - 4)) is not None:
                    out2(u - 4, j)

            pe.wait_ge(w_lo[V_], NG + 1)
            pe.wait_ge(d_small, 48)
            for j in range(5):
                if j < 4:
                    if j == 0:
                        pe.wait_ge(t2_evac, PAIRS)
                    transpose_x(4 + j)
                if j > 0:
                    for n, t in enumerate(o_tiles(j - 1)):
                        pe.wait_ge(av_done, t + 1)
                        if t >= 2:
                            pe.wait_ge(avT_lo, t - 1)
                        for c in range(KR):
                            mm = pe.transpose((b_z[:, 1, :], b_qk[0][:])[n][:, c * P:(c + 1) * P],
                                              av[:, n, c * P:(c + 1) * P], ident[:])
                        mm.then_inc(avT_ready, 1)
                if j < 4:
                    tiles = o_tiles(j)
                    cols = slice(tiles.start * P, tiles.stop * P)
                    pe.wait_ge(xT_lo, 4 + j + 1)
                    for m in range(KD):
                        mm = three(b_st[:, 1, m * D:m * D + len(tiles) * P],
                                   [(tuple(w[:, k, m * P:(m + 1) * P] for w in w1), tuple(x[:, k, cols] for x in x2))
                                    for k in range(KD)])
                    mm.then_inc(h_ready, 1)
                if j > 0:
                    if j > 1:
                        pe.wait_ge(u_added, j - 1)
                    for n, t in enumerate(o_tiles(j - 1)):
                        pe.wait_ge(avT_lo, t + 1)
                        mm = three(b_qk[1][:, n * D:(n + 1) * D],
                                   [(tuple(a[n][:, c, :] for a in avT), tuple(w[:, c, :] for w in uw))
                                    for c in range(KR)])
                    mm.then_inc(u_ready, 1)
                if j < 4:
                    pe.wait_ge(h_evac, j + 1)
                    if j > 0:
                        pe.wait_ge(lg_step, 3 * j - 2)
                    for n, t in enumerate(tiles):
                        for k in range(KD):
                            mm = pe.matmul(b_z[:, 0, n * EXPERTS:(n + 1) * EXPERTS], hT[:, k, n * P:(n + 1) * P],
                                           w2_s[:, k, :], start=(k == 0), stop=(k == KD - 1))
                    mm.then_inc(lg_ready, 1)
                    for n, t in enumerate(tiles):
                        if t >= 2:
                            pe.wait_ge(av_done, t - 1)
                        three(b_vo[n][:], [(tuple(x[:, k, t * P:(t + 1) * P] for x in x2),
                                            tuple(w[:, k, :] for w in vw)) for k in range(KD)]).then_inc(vx_ready, 1)


def lay_out(inputs):
    import numpy as np
    a = {k: np.asarray(v) for k, v in inputs.items()}
    w = np.zeros((NG + 1, 4, P, W), np.float32)
    for m, name in ((Q_, "L0_attn_W_Q"), (K_, "L0_attn_W_K"), (V_, "L0_attn_W_V")):
        w[:NG, m] = a[name].reshape(NG, G, E, KD, P).transpose(0, 4, 3, 1, 2).reshape(NG, P, W)
    w[:NG, O_] = a["L0_attn_W_O"].reshape(NG, G, D, E).transpose(0, 3, 1, 2).reshape(NG, P, W)
    wq = a["L0_xattn_Wq"].reshape(NHG, 1, SLOT, KD, P).repeat(2, axis=1)
    w[NG, Q_] = wq.transpose(4, 3, 0, 1, 2).reshape(P, W)
    wo = a["L0_xattn_Wout"].reshape(D, KD, P).transpose(2, 1, 0)
    w1 = a["L0_ffn_W1"].reshape(KD, P, D).transpose(1, 0, 2)
    w[NG, K_] = np.concatenate([wo, w1], axis=2).reshape(P, W)
    w[NG, V_] = a["L0_ffn_V"].reshape(EXPERTS * RANK, KD, P).transpose(2, 1, 0).reshape(P, W)
    w[NG, O_] = a["L0_ffn_U"].transpose(0, 2, 1).reshape(KR, P, D).transpose(1, 0, 2).reshape(P, W)
    wk, wv = a["L0_xattn_Wkv_expand"].reshape(2, D, XL)
    return {
        "x": a["x"].reshape(N, D),
        "xT": a["x"].transpose(2, 0, 1),
        "weights": w,
        "ctxT": a["ctx_512"].transpose(2, 0, 1),
        "wk_dup": wk.reshape(NHG, 1, SLOT, XL).repeat(2, axis=1).transpose(3, 0, 1, 2).reshape(XL, NHG, P),
        "wv": wv.T,
        "w2": a["L0_ffn_W2"].reshape(KD, P, EXPERTS).transpose(1, 0, 2),
        "b1": a["L0_ffn_b1"].reshape(KD, P).T,
        "b2": a["L0_ffn_b2"],
    }


def kernel(**inputs):
    import numpy as np
    import concourse.bacc as bacc
    from concourse.bass_utils import run_bass_kernel_spmd

    nc = bacc.Bacc("TRN2", target_bir_lowering=False, num_devices=1)
    arrays = {n: np.ascontiguousarray(a) for n, a in lay_out(inputs).items()}
    aps = {n: nc.dram_tensor(n, a.shape, mybir.dt.from_np(a.dtype), kind="ExternalInput").ap()
           for n, a in arrays.items()}
    out = nc.dram_tensor("out", (N, D), F32, kind="ExternalOutput").ap()
    build(nc, out=out, **aps)
    r = run_bass_kernel_spmd(nc, [arrays], core_ids=[0])
    return r.results[0]["out"].reshape(NB, S, D)
```

```python
from contextlib import ExitStack

import concourse.bass as bass
from concourse import mybir

ALU = mybir.AluOpType
ACT = mybir.ActivationFunctionType
AX_X = mybir.AxisListType.X
F32 = mybir.dt.float32
F32R = mybir.dt.float32r
BF16 = mybir.dt.bfloat16

NB, S, D = 16, 56, 256
N = NB * S
P = 128
TILES = N // P
KD = D // P
NH, E = 16, 128
G = 4
NG = NH // G
SLOT = 64
ROWS = SLOT + S
PAIRS = NB // 2
HALF = N // 2
XH, XE, XL = 16, 16, 64
HG = 4
NHG = XH // HG
HP = XH // 2
EXPERTS, RANK = 8, 64
KR = EXPERTS * RANK // P
EPS = 1e-5
MASKED = -1e30
W = 4 * D
Q_, K_, V_, O_ = range(4)
ATTN_SCALE = float(E) ** -0.5
XATTN_SCALE = float(XE) ** -0.5


def build(nc, x, xT, weights, ctxT, wk_dup, wv, w2, b1, b2, out):
    with ExitStack() as ctx:
        def sb(name, shape, dt=F32):
            return ctx.enter_context(nc.sbuf_tensor(name, shape, dt))

        def ps(name, shape):
            return ctx.enter_context(nc.psum_tensor(name, shape, F32))

        def sem(name):
            return ctx.enter_context(nc.semaphore(name))

        raw = sb("raw", [P, 4, W])
        w_h = sb("w_h", [P, 4, W], F32R)
        w_l = sb("w_l", [P, 4, W], F32R)
        xraw = sb("xraw", [P, KD, NB, S])
        xt_h = sb("xt_h", [P, KD, NB, SLOT], F32R)
        xt_l = sb("xt_l", [P, KD, NB, SLOT], F32R)
        qT = sb("qT", [P, N])
        kT = sb("kT", [P, N])
        v = sb("v", [P, PAIRS, G * E])
        prob = sb("prob", [P, 8, SLOT])
        probn = sb("probn", [P, 8, SLOT])
        pT = sb("pT", [P, PAIRS, 2 * S])
        mx = sb("mx", [P, 8])
        rs = sb("rs", [P, 8])
        rinv = sb("rinv", [P, 8])
        z_h = sb("z_h", [P, G, N], F32R)
        z_l = sb("z_l", [P, G, N], F32R)
        acc = sb("acc", [P, TILES, D])
        ident = sb("ident", [P, P])
        ident_b = sb("ident_b", [P, P], BF16)
        mask = sb("mask", [P, 8, SLOT], BF16)
        hmask = sb("hmask", [P, HG])
        neg_half = sb("neg_half", [P, 2])
        ctx_s = sb("ctx_s", [XL, NB, 2, SLOT])
        wk_s = sb("wk_s", [XL, NHG, P])
        wv_s = sb("wv_s", [XL, D])
        k2 = sb("k2", [P, NHG, PAIRS, HG, S])
        v2 = sb("v2", [P, NB, HP, 2 * XE])

        w2_s = sb("w2_s", [P, KD, EXPERTS])
        b1_s = sb("b1_s", [P, KD])
        b2_s = sb("b2_s", [P, EXPERTS])
        stats = sb("stats", [P, TILES, 6])
        mv = sb("mv", [P, TILES, 2])
        veps = sb("veps", [P, TILES])
        rstd = sb("rstd", [P, TILES])
        mx2 = sb("mx2", [P, 2, XH])
        rs2 = sb("rs2", [P, 2, XH])
        rinv2 = sb("rinv2", [P, 2, XH])
        hT = sb("hT", [P, KD, 2 * P])
        lg = sb("lg", [P, 2, EXPERTS])
        lgm = sb("lgm", [P, 2])
        lgs = sb("lgs", [P, 2])
        lgr = sb("lgr", [P, 2])
        alpha = sb("alpha", [P, 2, EXPERTS])
        av = sb("av", [P, 2, EXPERTS * RANK])

        def flat(t):
            return t[:].rearrange({3: "p a b -> p (a b)", 4: "p a b c -> p (a b c)"}[len(t.shape)])

        def halves(t, at):
            return flat(t)[:, at:at + KD * N].rearrange("p (k n) -> p k n", k=KD)

        x1 = [halves(t, 0) for t in (xt_h, xt_l)]
        z2 = [halves(t, 0) for t in (z_h, z_l)]
        x2 = [halves(t, KD * N) for t in (z_h, z_l)]
        q2 = flat(v)[:, 0:NHG * PAIRS * ROWS].rearrange("p (h a n) -> p h a n", h=NHG, a=PAIRS)
        p2 = [raw[:, i, :].rearrange("p (h m) -> p h m", m=SLOT) for i in range(2)]
        pT2 = [flat(t)[:, at:at + HP * ROWS].rearrange("p (h n) -> p h n", h=HP)
               for t, at in ((raw, V_ * W), (xraw, 0))]
        z2n = [prob[:, 4 * i:4 * i + 4, :].rearrange("p a m -> p (a m)") for i in range(2)]
        avT = [[flat(t)[:, i * 512:(i + 1) * 512].rearrange("p (c n) -> p c n", c=KR) for i in range(2)]
               for t in (xt_h, xt_l)]
        wq2 = [t[:, Q_, :].rearrange("p (k n) -> p k n", k=KD) for t in (w_h, w_l)]
        wout = [t[:, K_, :].rearrange("p (k n) -> p k n", k=KD)[:, :, 0:D] for t in (w_h, w_l)]
        w1 = [t[:, K_, :].rearrange("p (k n) -> p k n", k=KD)[:, :, D:2 * D] for t in (w_h, w_l)]
        vw = [t[:, V_, :].rearrange("p (k n) -> p k n", k=KD) for t in (w_h, w_l)]
        uw = [t[:, O_, :].rearrange("p (c n) -> p c n", c=KR) for t in (w_h, w_l)]

        b_qk = [ps(f"b_qk{i}", [P, 512]) for i in range(2)]
        b_st = ps("b_st", [P, 2, 512])
        b_s = b_st[:, 0, :]
        b_t = b_st[:, 1, :]
        b_z = ps("b_z", [P, 2, 512])
        b_vo = [ps(f"b_vo{i}", [P, 512]) for i in range(2)]

        avT_bank = [b[:].rearrange("p (c n) -> p c n", c=KR) for b in (b_vo[0], b_qk[0])]

        d_x, d_ctx, d_small = sem("d_x"), sem("d_ctx"), sem("d_small")
        d_xT = [sem(f"d_xT{c}") for c in range(2)]
        d_first = [sem(f"d_first{m}") for m in (Q_, K_)]
        d_w = [sem(f"d_w{m}") for m in range(4)]
        zeroed, consts = sem("zeroed"), sem("consts")
        x_hi_act, x_hi_dve, x_lo = sem("x_hi_act"), sem("x_hi_dve"), sem("x_lo")
        w_hi = [sem(f"w_hi{m}") for m in range(4)]
        w_lo = [sem(f"w_lo{m}") for m in range(4)]
        qk_ready, qk_evac = sem("qk_ready"), sem("qk_evac")
        s_ready, max_done, sub_done = sem("s_ready"), sem("max_done"), sem("sub_done")
        exp_done, sum_done, recip_done, pn_ready = (
            sem("exp_done"), sem("sum_done"), sem("recip_done"), sem("pn_ready"))
        t_ready, pt_act, pt_dve = sem("t_ready"), sem("pt_act"), sem("pt_dve")
        z_ready, z_hi, z_lo = sem("z_ready"), sem("z_hi"), sem("z_lo")
        v_ready, v_evac = sem("v_ready"), sem("v_evac")
        o_ready, o_added = sem("o_ready"), sem("o_added")
        c_ready, c_evac, k2_dve, k2_pool = sem("c_ready"), sem("c_evac"), sem("k2_dve"), sem("k2_pool")
        bn_done, aggr_done, ve_ready, rstd_ready, ln_done = (
            sem("bn_done"), sem("aggr_done"), sem("ve_ready"), sem("rstd_ready"), sem("ln_done"))
        xT_ready, xT_hi, xT_lo = sem("xT_ready"), sem("xT_hi"), sem("xT_lo")
        q2_zeroed, p2_zeroed = sem("q2_zeroed"), sem("p2_zeroed")
        q2_ready, q2_act, q2_dve = sem("q2_ready"), sem("q2_act"), sem("q2_dve")
        s2_ready, max2_done, sub2_done, exp2_done, sum2_done, recip2_done = (
            sem("s2_ready"), sem("max2_done"), sem("sub2_done"), sem("exp2_done"), sem("sum2_done"),
            sem("recip2_done"))
        t2_ready, t2_evac, pv2_ready, z2_norm = sem("t2_ready"), sem("t2_evac"), sem("pv2_ready"), sem("z2_norm")
        z2_ready, z2_hi, z2_lo = sem("z2_ready"), sem("z2_hi"), sem("z2_lo")
        out2_ready, out2_added = sem("out2_ready"), sem("out2_added")
        h_ready, h_evac, lg_ready, lg_step, lg_exp, alpha_done = (
            sem("h_ready"), sem("h_evac"), sem("lg_ready"), sem("lg_step"), sem("lg_exp"), sem("alpha_done"))
        vx_ready, av_done, avT_ready, avT_hi, avT_lo = (
            sem("vx_ready"), sem("av_done"), sem("avT_ready"), sem("avT_hi"), sem("avT_lo"))
        u_ready, u_added, stored = sem("u_ready"), sem("u_added"), sem("stored")

        def qk_cols(m, i):
            i = i if isinstance(i, slice) else slice(i, i + 1)
            return lambda t: t[:, m, :].rearrange("p (k n) -> p k n", k=KD)[:, :, i.start * E:i.stop * E]

        def half(m, i):
            return lambda t: t[:, m, i * W // 2:(i + 1) * W // 2]

        def w_landed(m, g):
            return (g + 1) * 16

        def ctx_uses(i):
            return range(3 * (i - 1), min(3 * i, 8)) if i > 0 else range(0)

        def out2_after(p):
            return {2: 0, 4: 1, 6: 2, 7: 3}.get(p)

        def staged(n):
            return flat(xraw)[:, (n % 4) * HALF:(n % 4 + 1) * HALF].rearrange("p (b m) -> p b m", m=S)

        def key_blocks(n, r):
            rows = slice(SLOT * r, SLOT * (r + 1))
            keys = staged(n)[rows].rearrange("p (a r) m -> p a r m", r=2)[:, :, r, :]
            return keys.unsqueeze(2).broadcast_to([SLOT, 4, HG, S])

        def head_blocks(r):
            return hmask[SLOT * r:SLOT * (r + 1), :].unsqueeze(1).unsqueeze(3).broadcast_to([SLOT, 4, HG, S])

        def value_bank(n):
            return b_qk[n % 2][:] if n < 10 else b_z[:, n % 2, :] if n < 12 else b_vo[n % 2][:]

        def xT_bank(n):
            return (b_st[:, n % 2, :] if n < 4 else b_vo[1][:]).rearrange("p (k n) -> p k n", k=KD)

        def o_tiles(j):
            return range(2 * j, min(2 * j + 2, TILES))

        block = ctx.enter_context(nc.Block())

        @block.sync
        def _(sp):
            first = [qk_cols(m, slice(0, 1))(raw) for m in (Q_, K_)]
            rest = [qk_cols(m, slice(1, G))(raw) for m in (Q_, K_)]
            cols = [weights[0, m].rearrange("p (k n) -> p k n", k=KD) for m in (Q_, K_)]
            xT_k = xT.rearrange("(k p) b s -> p k b s", p=P)
            sp.dma_start(first[Q_], cols[Q_][:, :, 0:E]).then_inc(d_first[Q_], 16)
            sp.dma_start(xraw[:, :, 0:NB // 2, :], xT_k[:, :, 0:NB // 2, :]).then_inc(d_xT[0], 16)
            sp.dma_start(first[K_], cols[K_][:, :, 0:E]).then_inc(d_first[K_], 16)
            sp.dma_start(xraw[:, :, NB // 2:, :], xT_k[:, :, NB // 2:, :]).then_inc(d_xT[1], 16)
            sp.dma_start(raw[:, V_, :], weights[0, V_]).then_inc(d_w[V_], 16)
            for m in (Q_, K_):
                sp.dma_start(rest[m], cols[m][:, :, E:G * E]).then_inc(d_w[m], 16)
            sp.dma_start(acc[:], x.rearrange("(t p) d -> p t d", p=P)).then_inc(d_x, 16)
            sp.dma_start(raw[:, O_, :], weights[0, O_]).then_inc(d_w[O_], 16)
            for r in range(2):
                sp.dma_start(ctx_s[:, :, r, 0:S], ctxT[:, :, 0:S]).then_inc(d_ctx, 16)
            sp.dma_start(wk_s[:], wk_dup).then_inc(d_ctx, 16)
            sp.dma_start(wv_s[:], wv).then_inc(d_ctx, 16)
            sp.dma_start(w2_s[:], w2).then_inc(d_small, 16)
            sp.dma_start(b1_s[:], b1).then_inc(d_small, 16)
            sp.dma_start(b2_s[:], b2.partition_broadcast(P)).then_inc(d_small, 16)
            with sp.Fori(1, NG + 1) as g:
                for m in range(4):
                    units = G if m in (Q_, K_) else 2
                    sp.wait_ge(w_hi[m], g * units)
                    sp.wait_ge(w_lo[m], g * units)
                    sp.dma_start(raw[:, m, :], weights[g, m]).then_inc(d_w[m], 16)
            for j in range(4):
                t = o_tiles(j)
                sp.wait_ge(ln_done, 8 + j + 1)
                sp.dma_start(out[t.start * P:t.stop * P].rearrange("(t p) d -> p t d", p=P),
                             acc[:, t.start:t.stop, :]).then_inc(stored, 16)
            sp.wait_ge(stored, 64)

        @block.gpsimd
        def _(pool):
            for t in (xt_h, xt_l):
                pool.memset(t[:, :, :, S:SLOT].bitcast(F32), 0.0).then_inc(zeroed, 1)
            pool.memset(ident[:], 0.0).then_inc(consts, 1)
            pool.memset(mask[:], 0.0).then_inc(consts, 1)
            pool.memset(probn[:], 0.0).then_inc(consts, 1)
            pool.memset(pT[:], 0.0).then_inc(zeroed, 1)
            pool.wait_ge(consts, 3)
            pool.affine_select(out=ident[:], in_=ident[:], compare_op=ALU.not_equal, fill=1.0, base=0,
                               pattern=[[-1, P]], channel_multiplier=1).then_inc(consts, 1)
            for r in range(2):
                pool.wait_ge(consts, 4 + r)
                rows = mask[SLOT * r:SLOT * (r + 1)]
                pool.affine_select(out=rows, in_=rows, compare_op=ALU.is_ge, fill=MASKED, base=0,
                                   pattern=[[0, 8], [-1, SLOT]], channel_multiplier=1).then_inc(consts, 1)
            pool.wait_ge(consts, 6)
            pool.tensor_copy(ident_b[:], ident[:]).then_inc(consts, 1)

            pool.memset(neg_half[:], -0.5).then_inc(consts, 1)
            pool.memset(ctx_s[:, :, 0, S:SLOT], 0.0).then_inc(consts, 1)
            pool.memset(ctx_s[:, :, 1, S:SLOT], 0.0).then_inc(consts, 1)
            pool.memset(hmask[:], 1.0).then_inc(consts, 1)
            for r in range(2):
                rows = hmask[SLOT * r:SLOT * (r + 1)]
                pool.wait_ge(consts, 11 + 2 * r)
                pool.affine_select(out=rows, in_=rows, compare_op=ALU.is_ge, fill=0.0, base=0,
                                   pattern=[[-XE, HG]], channel_multiplier=1).then_inc(consts, 1)
                pool.wait_ge(consts, 12 + 2 * r)
                pool.affine_select(out=rows, in_=rows, compare_op=ALU.is_ge, fill=0.0, base=XE - 1,
                                   pattern=[[XE, HG]], channel_multiplier=-1).then_inc(consts, 1)
            pool.wait_ge(consts, 15)
            pool.memset(v2[:], 0.0).then_inc(consts, 1)

            def norm(s, first=False):
                pool.wait_ge(recip_done, s + 1)
                if not first:
                    pool.wait_ge(t_ready, s)
                pool.tensor_tensor(probn[0:ROWS, :, 0:S], prob[0:ROWS, :, 0:S],
                                   rinv[0:ROWS, :].unsqueeze(2).broadcast_to([ROWS, 8, S]),
                                   ALU.mult).then_inc(pn_ready, 1)

            def split_lo(m, cols, count):
                pool.wait_ge(w_hi[m], count)
                pool.tensor_tensor(cols(w_l), cols(raw), cols(w_h).bitcast(F32), ALU.subtract).then_inc(w_lo[m], 1)

            def expand_keys(n):
                pool.wait_ge(c_evac, n + 1)
                hg, c = n % 4, n // 4
                pool.tensor_tensor(k2[0:SLOT, hg, 4 * c:4 * c + 4, :, :],
                                   key_blocks(n, 0), head_blocks(0), ALU.mult).then_inc(k2_pool, 1)

            def group(g, first=False):
                for i in range(G):
                    s = g * G + i
                    if i > 0 or not first:
                        for m in (Q_, K_):
                            pool.wait_ge(qk_ready, s * 4)
                            split_lo(m, qk_cols(m, (i - 1) % G), s + G)
                    if i == 2:
                        pool.wait_ge(v_ready, (g + 1) * PAIRS)
                        for h in range(2):
                            split_lo(V_, half(V_, h), (g + 1) * 2 + h + 1)
                    if i == 3:
                        if not first:
                            pool.wait_ge(o_ready, g * 4)
                        for h in range(2):
                            split_lo(O_, half(O_, h), g * 2 + h + 1)
                    norm(s, first and i == 0)
                    if first:
                        for n in ctx_uses(i):
                            expand_keys(n)

            group(0, first=True)
            with pool.Fori(1, NG) as g:
                group(g)
            for m in (Q_, K_):
                split_lo(m, qk_cols(m, G - 1), (NG + 1) * G)
            pool.wait_ge(z_ready, 2 * NH)
            pool.memset(q2, 0.0).then_inc(q2_zeroed, 1)

            def inverse_deviation(n):
                t = o_tiles(n % 4)
                pool.wait_ge(ve_ready, n + 1)
                pool.tensor_tensor(rstd[:, t.start:t.stop], veps[:, t.start:t.stop], neg_half[:, 0:len(t)],
                                   ALU.pow).then_inc(rstd_ready, 1)

            inverse_deviation(0)
            inverse_deviation(1)
            for m in (Q_, K_):
                pool.wait_ge(w_lo[m], (NG + 1) * G)
            for t in p2:
                pool.memset(t[:, :, S:SLOT], 0.0).then_inc(p2_zeroed, 1)
            inverse_deviation(2)
            inverse_deviation(3)
            for h in range(2):
                split_lo(O_, half(O_, h), NG * 2 + h + 1)
            for j in range(4):
                inverse_deviation(4 + j)
                pool.wait_ge(rstd_ready, 4 + j + 1)
                for t in o_tiles(j):
                    ins = pool.tensor_scalar(acc[:, t, :], acc[:, t, :], mv[:, t, 0:1], rstd[:, t:t + 1],
                                             ALU.subtract, ALU.mult)
                ins.then_inc(ln_done, 1)
            for n in range(8, 12):
                inverse_deviation(n)

        @block.scalar
        def _(act):
            def split_first(m):
                act.wait_ge(d_first[m], 16)
                cols = qk_cols(m, 0)
                act.copy(cols(w_h), cols(raw)).then_inc(w_hi[m], 1)

            def split_hi(m, cols, landed):
                act.wait_ge(d_w[m], landed)
                act.copy(cols(w_h), cols(raw)).then_inc(w_hi[m], 1)

            split_first(Q_)
            for c in range(2):
                act.wait_ge(d_xT[c], 16)
                b = slice(c * NB // 2, (c + 1) * NB // 2)
                act.copy(xt_h[:, 0, b, 0:S], xraw[:, 0, b]).then_inc(x_hi_act, 1)
                if c == 0:
                    split_first(K_)

            def evac_qk(s, n):
                act.wait_ge(qk_ready, s * 4 + n + 1)
                dst = (qT, kT)[n % 2]
                act.copy(dst[:, (n // 2) * HALF:(n // 2 + 1) * HALF], b_qk[n % 2][:, 0:HALF]).then_inc(qk_evac, 1)

            def evac_pT(s):
                act.wait_ge(t_ready, s + 1)
                act.copy(pT[0:S, :, 0:S],
                         b_t[0:S, :].rearrange("p (a m) -> p a m", m=SLOT)[:, :, 0:S]).then_inc(pt_act, 1)

            def exp(s):
                act.wait_ge(sub_done, s + 1)
                act.activation(prob[0:ROWS, :, 0:S], prob[0:ROWS, :, 0:S], ACT.Exp,
                               scale=ATTN_SCALE).then_inc(exp_done, 1)

            def evac_z_hi(s, i):
                for c in range(2):
                    act.wait_ge(z_ready, s * 2 + c + 1)
                    act.copy(z_h[:, i, c * HALF:(c + 1) * HALF], b_z[:, c, 0:HALF]).then_inc(z_hi, 1)

            def stage_keys(n):
                act.wait_ge(c_ready, n + 1)
                if n < 4:
                    act.wait_ge(x_lo, 4)
                else:
                    act.wait_ge(k2_dve, n - 3)
                    act.wait_ge(k2_pool, n - 3)
                act.copy(staged(n), b_vo[n % 2][:, 0:HALF].rearrange("p (b m) -> p b m", m=S)).then_inc(c_evac, 1)

            def place_values(n):
                act.wait_ge(c_ready, n + 1)
                b = 2 * (n - 8)
                for r in range(2):
                    src = value_bank(n)[SLOT * r:SLOT * r + S, :].rearrange("p (b h r e) -> p b h r e", b=2, h=HP, r=2)
                    ins = act.copy(v2[SLOT * r:SLOT * r + S, b:b + 2, :, r * XE:(r + 1) * XE], src[:, :, :, r, :])
                ins.then_inc(c_evac, 1)

            def group(g, first=False):
                for i in range(G):
                    s = g * G + i
                    begin = first and i == 0
                    if not begin:
                        act.wait_ge(s_ready, s)
                    for n in range(4):
                        evac_qk(s, n)
                        if begin and n in (1, 2):
                            split_hi(V_, half(V_, n - 1), w_landed(V_, 0))
                        if n < 2 and not (first and i <= 1):
                            split_hi(n, qk_cols(n, (i - 1) % G), w_landed(n, g if i == 0 else g + 1))
                        if n == 2 and i == 2:
                            act.wait_ge(v_ready, (g + 1) * PAIRS)
                            split_hi(V_, half(V_, 0), w_landed(V_, g + 1))
                        if n == 2 and i == 3:
                            if not first:
                                act.wait_ge(o_ready, g * 4)
                            split_hi(O_, half(O_, 0), w_landed(O_, g))
                        if first and n in (1, 3) and i > 0:
                            stage_keys(ctx_uses(i)[n // 2])
                    if begin:
                        for m in (Q_, K_):
                            split_hi(m, qk_cols(m, 1), w_landed(m, 0))
                    else:
                        evac_pT(s - 1)
                    if i == 2:
                        split_hi(V_, half(V_, 1), w_landed(V_, g + 1))
                    if i == 3:
                        split_hi(O_, half(O_, 1), w_landed(O_, g))
                    exp(s)
                    if not begin:
                        evac_z_hi(s - 1, (i - 1) % G)
                    if i == 0:
                        for j in range(PAIRS):
                            act.wait_ge(v_ready, g * PAIRS + j + 1)
                            act.copy(v[0:ROWS, j, :], b_vo[j % 2][0:ROWS, :]).then_inc(v_evac, 1)
                    if begin:
                        for h in range(2, G):
                            for m in (Q_, K_):
                                split_hi(m, qk_cols(m, h), w_landed(m, 0))
                    if first and i == 1:
                        for m in (Q_, K_):
                            split_hi(m, qk_cols(m, 0), w_landed(m, 1))
                    if first:
                        for n in ctx_uses(i)[2:]:
                            stage_keys(n)

            group(0, first=True)
            with act.Fori(1, NG) as g:
                group(g)
            for m in (Q_, K_):
                split_hi(m, qk_cols(m, G - 1), w_landed(m, NG))
            evac_pT(NH - 1)
            evac_z_hi(NH - 1, G - 1)

            def evac_xT(n, dst):
                t = o_tiles(n % 4)
                act.wait_ge(xT_ready, n + 1)
                act.copy(dst[0][:, :, t.start * P:t.stop * P], xT_bank(n)[:, :, 0:len(t) * P]).then_inc(xT_hi, 1)

            def evac_q2(n):
                hg, c = n % 4, n // 4
                act.wait_ge(q2_ready, n + 1)
                act.copy(q2[0:SLOT, hg, 4 * c:4 * c + 4, 0:S],
                         b_qk[n % 2][0:SLOT, 0:HALF].rearrange("p (a r m) -> p a r m", r=2, m=S)[:, :, 0, :]
                         ).then_inc(q2_act, 1)

            for n in range(8, 12):
                place_values(n)
            evac_xT(0, x1)
            evac_xT(1, x1)
            act.wait_ge(q2_zeroed, 1)
            evac_q2(0)
            evac_q2(1)
            evac_xT(2, x1)
            evac_q2(2)
            evac_q2(3)
            evac_xT(3, x1)
            place_values(12)
            place_values(13)

            def relu(j):
                cols = len(o_tiles(j)) * P
                act.wait_ge(h_ready, j + 1)
                for m in range(KD):
                    ins = act.activation(hT[:, m, 0:cols], b_vo[1][:, m * D:m * D + cols], ACT.Relu,
                                         bias=b1_s[:, m:m + 1])
                ins.then_inc(h_evac, 1)

            def logits_exp(j):
                nt = len(o_tiles(j))
                act.wait_ge(lg_step, 3 * j + 3)
                act.activation(lg[:, 0:nt, :], lg[:, 0:nt, :], ACT.Exp).then_inc(lg_exp, 1)

            def evac_avT(j):
                for n, t in enumerate(o_tiles(j)):
                    act.wait_ge(avT_ready, t + 1)
                    act.copy(avT[0][n], avT_bank[n]).then_inc(avT_hi, 1)

            def evac_pT2(p):
                act.wait_ge(t2_ready, p + 1)
                if p >= 2:
                    act.wait_ge(pv2_ready, p - 1)
                act.copy(pT2[p % 2][0:ROWS, :, :],
                         b_st[0:ROWS, :, :].rearrange("p a (h n) -> p (a h) n", n=P)[:, :, 0:ROWS]
                         ).then_inc(t2_evac, 1)

            for u in range(PAIRS + 3):
                if 2 <= u <= PAIRS:
                    evac_pT2(u - 1)
                if u < 2:
                    place_values(14 + u)
                    evac_q2(4 + 2 * u)
                if u < PAIRS:
                    act.wait_ge(sub2_done, u + 1)
                    act.activation(p2[u % 2][0:ROWS, :, 0:S], p2[u % 2][0:ROWS, :, 0:S], ACT.Exp,
                                   scale=XATTN_SCALE).then_inc(exp2_done, 1)
                if u < 2:
                    evac_q2(5 + 2 * u)
                if u == 1:
                    evac_pT2(0)
                if u == 3:
                    for h in range(2):
                        split_hi(O_, half(O_, h), w_landed(O_, NG))
                if 0 <= u - 3 < PAIRS:
                    p = u - 3
                    act.wait_ge(z2_ready, p + 1)
                    for k in range(KD):
                        ins = act.copy(z2[0][:, k, p * 2 * S:(p + 1) * 2 * S].rearrange("p (r m) -> p r m", r=2),
                                       b_qk[0][:, k * D:k * D + P].rearrange("p (r m) -> p r m", r=2)[:, :, 0:S])
                    ins.then_inc(z2_hi, 1)
                if u == PAIRS - 1:
                    act.wait_ge(d_small, 48)
                    evac_xT(4, x2)
                if u == PAIRS:
                    relu(0)
                if u == PAIRS + 1:
                    logits_exp(0)
            evac_xT(5, x2)
            evac_avT(0)
            for j in range(1, 4):
                relu(j)
                logits_exp(j)
                if j < 3:
                    evac_xT(5 + j, x2)
                evac_avT(j)

        @block.vector
        def _(dve):
            def split_lo(m, cols, count):
                dve.wait_ge(w_hi[m], count)
                dve.tensor_tensor(cols(w_l), cols(raw), cols(w_h).bitcast(F32), ALU.subtract).then_inc(w_lo[m], 1)

            def batches(c):
                return slice(c * NB // 2, (c + 1) * NB // 2)

            def split_x_hi(c):
                dve.wait_ge(d_xT[c], 16)
                dve.tensor_copy(xt_h[:, 1, batches(c), 0:S], xraw[:, 1, batches(c)]).then_inc(x_hi_dve, 1)

            def split_x_lo(c):
                for k, done in ((0, x_hi_act), (1, x_hi_dve)):
                    dve.wait_ge(done, c + 1)
                    dve.tensor_tensor(xt_l[:, k, batches(c), 0:S], xraw[:, k, batches(c)],
                                      xt_h[:, k, batches(c), 0:S].bitcast(F32), ALU.subtract).then_inc(x_lo, 1)

            split_lo(Q_, qk_cols(Q_, 0), 1)
            split_x_hi(0)
            split_x_lo(0)
            split_lo(K_, qk_cols(K_, 0), 1)
            split_x_hi(1)
            split_x_lo(1)
            for h in range(2):
                split_lo(V_, half(V_, h), h + 1)
            for m in (Q_, K_):
                split_lo(m, qk_cols(m, 1), 2)

            def evac_pT(s):
                dve.wait_ge(t_ready, s + 1)
                dve.tensor_copy(pT[SLOT:ROWS, :, S:2 * S],
                                b_t[SLOT:ROWS, :].rearrange("p (a m) -> p a m", m=SLOT)[:, :, 0:S]).then_inc(pt_dve, 1)

            def center(s, first=False):
                dve.wait_ge(s_ready, s + 1)
                scores = b_s[0:ROWS, :].rearrange("p (a m) -> p a m", m=SLOT)[:, :, 0:S]
                dve.tensor_reduce(mx[0:ROWS, :], scores, AX_X, ALU.max).then_inc(max_done, 1)
                dve.wait_ge(max_done, s + 1)
                if not first:
                    dve.wait_ge(pn_ready, s)
                dve.tensor_tensor(prob[0:ROWS, :, 0:S], scores,
                                  mx[0:ROWS, :].unsqueeze(2).broadcast_to([ROWS, 8, S]),
                                  ALU.subtract).then_inc(sub_done, 1)

            def row_sums(s):
                dve.wait_ge(exp_done, s + 1)
                dve.tensor_reduce(rs[0:ROWS, :], prob[0:ROWS, :, 0:S], AX_X, ALU.add).then_inc(sum_done, 1)
                dve.wait_ge(sum_done, s + 1)
                dve.reciprocal(rinv[0:ROWS, :], rs[0:ROWS, :]).then_inc(recip_done, 1)

            def evac_z_lo(s, i):
                for c in range(2):
                    dve.wait_ge(z_hi, s * 2 + c + 1)
                    cols = slice(c * HALF, (c + 1) * HALF)
                    dve.tensor_tensor(z_l[:, i, cols], b_z[:, c, 0:HALF], z_h[:, i, cols].bitcast(F32),
                                      ALU.subtract).then_inc(z_lo, 1)

            def add_o_step(g, j):
                dve.wait_ge(o_ready, g * 4 + j + 1)
                t = o_tiles(j)
                a = acc[:, t.start:t.stop, :]
                dve.tensor_tensor(a, b_vo[j % 2][:, 0:len(t) * D].rearrange("p (t d) -> p t d", d=D), a,
                                  ALU.add).then_inc(o_added, 1)

            def add_o(g):
                for j in range(4):
                    add_o_step(g, j)

            def expand_keys(n):
                hg, c = n % 4, n // 4
                dve.wait_ge(c_evac, n + 1)
                dve.tensor_tensor(k2[SLOT:P, hg, 4 * c:4 * c + 4, :, :],
                                  key_blocks(n, 1), head_blocks(1), ALU.mult).then_inc(k2_dve, 1)

            def group(g, first=False):
                for i in range(G):
                    s = g * G + i
                    begin = first and i == 0
                    if not begin:
                        evac_pT(s - 1)
                    center(s, begin)
                    row_sums(s)
                    if not begin:
                        evac_z_lo(s - 1, (i - 1) % G)
                    if begin:
                        for h in range(2, G):
                            for m in (Q_, K_):
                                split_lo(m, qk_cols(m, h), h + 1)
                    if first:
                        if i == 1:
                            dve.wait_ge(consts, 15)
                        for n in ctx_uses(i):
                            expand_keys(n)
                    if i == 0 and not first:
                        add_o(g - 1)

            dve.wait_ge(zeroed, 3)
            dve.wait_ge(d_x, 16)
            group(0, first=True)
            with dve.Fori(1, NG) as g:
                group(g)
            evac_pT(NH - 1)
            evac_z_lo(NH - 1, G - 1)

            def moments(layer, j, added):
                sem_, count = added
                tiles = o_tiles(j)
                dve.wait_ge(sem_, count)
                for t in tiles:
                    dve.bn_stats(stats[:, t, :], acc[:, t, :]).then_inc(bn_done, 1)
                for t in tiles:
                    dve.wait_ge(bn_done, layer * TILES + t + 1)
                    dve.bn_aggr(mv[:, t, :], stats[:, t, :]).then_inc(aggr_done, 1)
                dve.wait_ge(aggr_done, layer * TILES + tiles.stop)
                dve.tensor_scalar(veps[:, tiles.start:tiles.stop], mv[:, tiles.start:tiles.stop, 1], EPS, None,
                                  ALU.add).then_inc(ve_ready, 1)

            def normalize(layer, j):
                dve.wait_ge(rstd_ready, layer * 4 + j + 1)
                for t in o_tiles(j):
                    ins = dve.tensor_scalar(acc[:, t, :], acc[:, t, :], mv[:, t, 0:1], rstd[:, t:t + 1],
                                            ALU.subtract, ALU.mult)
                ins.then_inc(ln_done, 1)

            def evac_xT(n, dst):
                t = o_tiles(n % 4)
                cols = slice(t.start * P, t.stop * P)
                dve.wait_ge(xT_hi, n + 1)
                dve.tensor_tensor(dst[1][:, :, cols], xT_bank(n)[:, :, 0:len(t) * P],
                                  dst[0][:, :, cols].bitcast(F32), ALU.subtract).then_inc(xT_lo, 1)

            def evac_q2(n):
                hg, c = n % 4, n // 4
                dve.wait_ge(q2_ready, n + 1)
                dve.tensor_copy(q2[SLOT:P, hg, 4 * c:4 * c + 4, SLOT:ROWS],
                                b_qk[n % 2][SLOT:P, 0:HALF].rearrange("p (a r m) -> p a r m", r=2, m=S)[:, :, 1, :]
                                ).then_inc(q2_dve, 1)

            def first_norm(j):
                add_o_step(NG - 1, j)
                moments(0, j, (o_added, NG * 4 - 4 + j + 1))

            dve.wait_ge(o_added, NG * 4 - 4)
            first_norm(0)
            first_norm(1)
            normalize(0, 0)
            normalize(0, 1)
            evac_xT(0, x1)
            evac_xT(1, x1)
            first_norm(2)
            normalize(0, 2)
            dve.wait_ge(q2_zeroed, 1)
            evac_q2(0)
            evac_q2(1)
            evac_xT(2, x1)
            first_norm(3)
            normalize(0, 3)
            evac_q2(2)
            evac_q2(3)
            evac_xT(3, x1)

            def experts_out(j):
                t = o_tiles(j)
                a = acc[:, t.start:t.stop, :]
                dve.wait_ge(u_ready, j + 1)
                dve.tensor_tensor(a, b_st[:, j % 2, 0:len(t) * D].rearrange("p (t d) -> p t d", d=D), a,
                                  ALU.add).then_inc(u_added, 1)
                moments(2, j, (u_added, j + 1))

            def weigh(j):
                tiles = o_tiles(j)
                nt = len(tiles)
                dve.wait_ge(lg_ready, j + 1)
                dve.tensor_tensor(lg[:, 0:nt, :], b_vo[1][:, 0:nt * EXPERTS].rearrange("p (t e) -> p t e", e=EXPERTS),
                                  b2_s[:].unsqueeze(1).broadcast_to([P, nt, EXPERTS]), ALU.add).then_inc(lg_step, 1)
                dve.wait_ge(lg_step, 3 * j + 1)
                dve.tensor_reduce(lgm[:, 0:nt], lg[:, 0:nt, :], AX_X, ALU.max).then_inc(lg_step, 1)
                dve.wait_ge(lg_step, 3 * j + 2)
                dve.tensor_tensor(lg[:, 0:nt, :], lg[:, 0:nt, :],
                                  lgm[:, 0:nt].unsqueeze(2).broadcast_to([P, nt, EXPERTS]),
                                  ALU.subtract).then_inc(lg_step, 1)
                dve.wait_ge(lg_exp, j + 1)
                dve.tensor_reduce(lgs[:, 0:nt], lg[:, 0:nt, :], AX_X, ALU.add).then_inc(alpha_done, 1)
                dve.wait_ge(alpha_done, 3 * j + 1)
                dve.reciprocal(lgr[:, 0:nt], lgs[:, 0:nt]).then_inc(alpha_done, 1)
                dve.wait_ge(alpha_done, 3 * j + 2)
                dve.tensor_tensor(alpha[:, 0:nt, :], lg[:, 0:nt, :],
                                  lgr[:, 0:nt].unsqueeze(2).broadcast_to([P, nt, EXPERTS]),
                                  ALU.mult).then_inc(alpha_done, 1)
                dve.wait_ge(alpha_done, 3 * j + 3)
                for n, t in enumerate(tiles):
                    dve.wait_ge(vx_ready, t + 1)
                    if t >= 2:
                        dve.wait_ge(avT_ready, t - 1)
                    dve.tensor_tensor(av[:, n, :].rearrange("p (e r) -> p e r", r=RANK),
                                      b_z[:, n, :].rearrange("p (e r) -> p e r", r=RANK),
                                      alpha[:, n, :].unsqueeze(2).broadcast_to([P, EXPERTS, RANK]),
                                      ALU.mult).then_inc(av_done, 1)

            def evac_avT(j):
                for n, t in enumerate(o_tiles(j)):
                    dve.wait_ge(avT_hi, t + 1)
                    dve.tensor_tensor(avT[1][n], avT_bank[n], avT[0][n].bitcast(F32), ALU.subtract).then_inc(avT_lo, 1)

            dve.wait_ge(p2_zeroed, 2)
            dve.wait_ge(pn_ready, NH)
            for u in range(PAIRS + 4):
                if u < PAIRS:
                    sc = b_z[0:ROWS, :, :].rearrange("p a (h m) -> p (a h) m", m=SLOT)[:, :, 0:S]
                    m_ = mx2[0:ROWS, u % 2, :]
                    dve.wait_ge(s2_ready, u + 1)
                    dve.tensor_reduce(m_, sc, AX_X, ALU.max).then_inc(max2_done, 1)
                    dve.wait_ge(max2_done, u + 1)
                    if u >= 2:
                        dve.wait_ge(t2_ready, u - 1)
                    dve.tensor_tensor(p2[u % 2][0:ROWS, :, 0:S], sc,
                                      m_.unsqueeze(2).broadcast_to([ROWS, XH, S]), ALU.subtract).then_inc(sub2_done, 1)
                if u < 2:
                    evac_q2(4 + 2 * u)
                    evac_q2(5 + 2 * u)
                if 0 <= u - 2 < PAIRS:
                    p = u - 2
                    dve.wait_ge(pv2_ready, p + 1)
                    dve.wait_ge(recip2_done, p + 1)
                    if p >= 2:
                        dve.wait_ge(z2_ready, p - 1)
                    dve.tensor_tensor(z2n[p % 2][0:ROWS, :].rearrange("p (h e) -> p h e", e=XE),
                                      b_vo[0][0:ROWS, 0:D].rearrange("p (h e) -> p h e", e=XE),
                                      rinv2[0:ROWS, p % 2, :].unsqueeze(2).broadcast_to([ROWS, XH, XE]),
                                      ALU.mult).then_inc(z2_norm, 1)
                if 0 <= u - 1 < PAIRS:
                    p = u - 1
                    dve.wait_ge(exp2_done, p + 1)
                    dve.tensor_reduce(rs2[0:ROWS, p % 2, :], p2[p % 2][0:ROWS, :, 0:S], AX_X,
                                      ALU.add).then_inc(sum2_done, 1)
                    dve.wait_ge(sum2_done, p + 1)
                    dve.reciprocal(rinv2[0:ROWS, p % 2, :], rs2[0:ROWS, p % 2, :]).then_inc(recip2_done, 1)
                if 0 <= u - 3 < PAIRS:
                    p = u - 3
                    dve.wait_ge(z2_hi, p + 1)
                    for k in range(KD):
                        cols = slice(p * 2 * S, (p + 1) * 2 * S)
                        ins = dve.tensor_tensor(
                            z2[1][:, k, cols].rearrange("p (r m) -> p r m", r=2),
                            b_qk[0][:, k * D:k * D + P].rearrange("p (r m) -> p r m", r=2)[:, :, 0:S],
                            z2[0][:, k, cols].rearrange("p (r m) -> p r m", r=2).bitcast(F32), ALU.subtract)
                    ins.then_inc(z2_lo, 1)
                if 0 <= u - 4 and (j := out2_after(u - 4)) is not None:
                    t = o_tiles(j)
                    a = acc[:, t.start:t.stop, :]
                    dve.wait_ge(out2_ready, j + 1)
                    dve.wait_ge(xT_ready, j + 1)
                    dve.tensor_tensor(a, b_qk[1][:, 0:len(t) * D].rearrange("p (t d) -> p t d", d=D), a,
                                      ALU.add).then_inc(out2_added, 1)
                    moments(1, j, (out2_added, j + 1))
                if u == PAIRS - 1:
                    dve.wait_ge(d_small, 48)
                    evac_xT(4, x2)
                if u == PAIRS + 1:
                    weigh(0)
                    evac_xT(5, x2)
            evac_avT(0)
            for j in range(1, 4):
                weigh(j)
                if j < 3:
                    evac_xT(5 + j, x2)
                experts_out(j - 1)
                evac_avT(j)
                normalize(2, j - 1)
            experts_out(3)
            normalize(2, 3)

        @block.tensor
        def _(pe):
            def three(out_, terms, start=True, stop=True, **kw):
                last = None
                steps = [(a, b) for (ah, al), (bh, bl) in terms for a, b in ((ah, bh), (al, bh), (ah, bl))]
                for n, (a, b) in enumerate(steps):
                    last = pe.matmul(out_, a, b, start=(start and n == 0), stop=(stop and n == len(steps) - 1), **kw)
                return last

            def qk(s, i, first=False, between=lambda c: None):
                for c in range(2):
                    batches = slice(c * NB // 2, (c + 1) * NB // 2)
                    for m in (Q_, K_):
                        if c == 0:
                            pe.wait_ge(w_lo[m], s + 1)
                        wh, wl = (qk_cols(m, i)(t) for t in (w_h, w_l))
                        if not first or c > 0:
                            pe.wait_ge(qk_evac, s * 4 + 2 * c + m - 1)
                        for k in range(KD):
                            if first and m == Q_:
                                pe.wait_ge(x_lo, 2 * c + k + 1)
                            mm = three(b_qk[m][:, 0:HALF],
                                       [((wh[:, k, :], wl[:, k, :]),
                                         (xt_h[:, k, batches, 0:S], xt_l[:, k, batches, 0:S]))],
                                       start=(k == 0), stop=(k == KD - 1))
                        mm.then_inc(qk_ready, 1)
                    between(c)

            def transposes(s):
                pe.wait_ge(pn_ready, s + 1)
                for t in range(4):
                    mm = pe.transpose(b_t[0:ROWS, t * P:t * P + ROWS],
                                      probn[0:ROWS, 2 * t:2 * t + 2, :].rearrange("p a m -> p (a m)")[:, 0:ROWS],
                                      ident[0:ROWS, 0:ROWS])
                mm.then_inc(t_ready, 1)

            def scores(s, first=False):
                if not first:
                    pe.wait_ge(sub_done, s)
                pe.matmul(b_s, ident_b[:], mask[:].rearrange("p a m -> p (a m)"), start=True, stop=False,
                          skip_group_check=True)
                for t, c, r in ((t, c, r) for t in range(4) for c in range(2) for r in range(2)):
                    b = 4 * t + 2 * r + c
                    if b == 0:
                        pe.wait_ge(qk_evac, s * 4 + 2)
                    if b == NB // 2:
                        pe.wait_ge(qk_evac, s * 4 + 4)
                    cols = slice(b * S, (b + 1) * S)
                    mm = pe.matmul(b_s[SLOT * r:SLOT * r + S, t * P + SLOT * c:t * P + SLOT * c + S],
                                   qT[:, cols], kT[:, cols], start=False, stop=True, skip_group_check=True)
                mm.then_inc(s_ready, 1)

            def pv(s, i, g, first=False):
                pe.wait_ge(pt_act, s + 1)
                pe.wait_ge(pt_dve, s + 1)
                pe.wait_ge(v_evac, (g + 1) * PAIRS)
                for c in range(2):
                    if not first:
                        pe.wait_ge(z_hi, s * 2 + c - 1)
                        pe.wait_ge(z_lo, s * 2 + c - 1)
                    for p in range(4):
                        pair = 4 * c + p
                        mm = pe.matmul(b_z[:, c, p * 2 * S:(p + 1) * 2 * S], v[0:ROWS, pair, i * E:(i + 1) * E],
                                       pT[0:ROWS, pair, :], start=True, stop=True)
                    mm.then_inc(z_ready, 1)

            def values(g):
                pe.wait_ge(w_hi[V_], 2 * g + 2)
                pe.wait_ge(w_lo[V_], 2 * g + 2)
                wh, wl = (t[:, V_, :].rearrange("p (k n) -> p k n", k=KD) for t in (w_h, w_l))
                for j in range(PAIRS):
                    if j >= 2:
                        pe.wait_ge(v_evac, g * PAIRS + j - 1)
                    xs = [tuple(t[:, k, 2 * j:2 * j + 2, :].rearrange("p b s -> p (b s)")[:, 0:ROWS]
                                for t in (xt_h, xt_l)) for k in range(KD)]
                    three(b_vo[j % 2][0:ROWS, :],
                          [(xs[k], (wh[:, k, :], wl[:, k, :])) for k in range(KD)]).then_inc(v_ready, 1)

            def project_heads(g, j, heads, first=True, last=True):
                wh, wl = (t[:, O_, :].rearrange("p (h n) -> p h n", h=G) for t in (w_h, w_l))
                for n, t in enumerate(o_tiles(j)):
                    cols = slice(t * P, (t + 1) * P)
                    whole = first and last
                    mm = three(b_vo[j % 2][:, n * D:(n + 1) * D],
                               [((z_h[:, h, cols], z_l[:, h, cols]), (wh[:, h, :], wl[:, h, :])) for h in heads],
                               start=first and (whole or n == 0), stop=last, skip_group_check=not whole)
                if last:
                    mm.then_inc(o_ready, 1)

            def project(g):
                pe.wait_ge(w_lo[O_], 2 * g + 2)
                pe.wait_ge(z_lo, (g + 1) * G * 2)
                for j in range(4):
                    if j < 2:
                        pe.wait_ge(v_evac, (g + 1) * PAIRS + PAIRS - 1 + j)
                    else:
                        pe.wait_ge(o_added, g * 4 + j - 1)
                    project_heads(g, j, range(G))

            pe.wait_ge(consts, 7)
            pe.wait_ge(zeroed, 2)

            def group(g, first=False):
                for i in range(G):
                    s = g * G + i
                    begin = first and i == 0
                    if first and i == 1:
                        pe.wait_ge(d_ctx, 64)
                        pe.wait_ge(consts, 10)
                    if first and i > 0:
                        qk(s, i, between=lambda c: latent(ctx_uses(i)[c]))
                    else:
                        qk(s, i, begin)
                    if not begin:
                        transposes(s - 1)
                    scores(s, begin)
                    if i == 0:
                        if not first:
                            pv(s - 1, G - 1, g - 1)
                        values(g)
                        if not first:
                            project(g - 1)
                    else:
                        pv(s - 1, i - 1, g, first and i == 1)
                        if first:
                            for n in ctx_uses(i)[2:]:
                                latent(n)

            def latent(n):
                if n < 2:
                    pe.wait_ge(v_evac, PAIRS - 1 + n)
                elif n < 8 or n >= 14:
                    pe.wait_ge(c_evac, n - 1)
                elif n >= 12:
                    pe.wait_ge(o_added, NG * 4 - 13 + n)
                if n < 8:
                    hg, c = n % 4, n // 4
                    mm = pe.matmul(b_vo[n % 2][:, 0:HALF], wk_s[:, hg, :], ctx_s[:, 8 * c:8 * c + 8, 0, 0:S],
                                   start=True, stop=True)
                else:
                    for i in range(2):
                        b = 2 * (n - 8) + i
                        mm = pe.matmul(value_bank(n)[0:ROWS, i * D:(i + 1) * D],
                                       ctx_s[:, b, :, :].rearrange("p r m -> p (r m)")[:, 0:ROWS], wv_s[:],
                                       start=True, stop=True)
                mm.then_inc(c_ready, 1)

            group(0, first=True)
            pe.wait_ge(c_evac, 8)
            with pe.Fori(1, NG) as g:
                group(g)

            pe.wait_ge(w_lo[O_], 2 * NG)
            pe.wait_ge(z_lo, (NH - 2) * 2)
            for j in range(2):
                project_heads(NG - 1, j, range(0, 2), last=False)
            transposes(NH - 1)
            pe.wait_ge(z_lo, (NH - 1) * 2)
            for j in range(2):
                project_heads(NG - 1, j, range(2, 3), first=False, last=False)
            pv(NH - 1, G - 1, NG - 1)
            latent(8)
            latent(9)

            def transpose_x(n):
                pe.wait_ge(ln_done, n + 1)
                if n in (2, 3):
                    pe.wait_ge(xT_lo, n - 1)
                elif n > 4:
                    pe.wait_ge(lg_step, 3 * (n - 5) + 1)
                for i, t in enumerate(o_tiles(n % 4)):
                    for k in range(KD):
                        mm = pe.transpose(xT_bank(n)[:, k, i * P:(i + 1) * P],
                                          acc[:, t, k * P:(k + 1) * P], ident[:])
                mm.then_inc(xT_ready, 1)

            def queries(n):
                hg, c = n % 4, n // 4
                pe.wait_ge(xT_lo, 2 * c + 2)
                if n >= 2:
                    pe.wait_ge(q2_act, n - 1)
                    pe.wait_ge(q2_dve, n - 1)
                cols = slice(c * HALF, (c + 1) * HALF)
                three(b_qk[n % 2][:, 0:HALF],
                      [(tuple(w[:, k, hg * P:(hg + 1) * P] for w in wq2), tuple(x[:, k, cols] for x in x1))
                       for k in range(KD)]).then_inc(q2_ready, 1)

            pe.wait_ge(z_lo, NH * 2)
            for j in range(2):
                project_heads(NG - 1, j, range(3, 4), first=False)
            latent(10)
            latent(11)
            pe.wait_ge(o_added, NG * 4 - 3)
            project_heads(NG - 1, 2, range(G))
            transpose_x(0)
            transpose_x(1)
            pe.wait_ge(o_added, NG * 4 - 2)
            project_heads(NG - 1, 3, range(G))
            pe.wait_ge(w_lo[Q_], (NG + 1) * G)
            queries(0)
            queries(1)
            transpose_x(2)
            queries(2)
            queries(3)
            transpose_x(3)
            latent(12)
            latent(13)

            def scores2(p):
                if p == 0:
                    pe.wait_ge(c_evac, 12)
                pe.wait_ge(q2_act, 4 * (p // 4) + 4)
                pe.wait_ge(q2_dve, 4 * (p // 4) + 4)
                if p > 0:
                    pe.wait_ge(sub2_done, p)
                for half in range(2):
                    pe.matmul(b_z[:, half, :], ident_b[:], mask[:].rearrange("p a m -> p (a m)"), start=True,
                              stop=False, skip_group_check=True)
                    for i in range(2):
                        hg = 2 * half + i
                        mm = pe.matmul(b_z[0:ROWS, half, i * D:(i + 1) * D].rearrange("p (h m) -> p h m", m=SLOT)[:, :, 0:S],
                                       q2[:, hg, p, :], k2[:, hg, p, :, :], start=False, stop=True,
                                       skip_group_check=True)
                mm.then_inc(s2_ready, 1)

            def transposes2(p):
                pe.wait_ge(exp2_done, p + 1)
                if p > 0:
                    pe.wait_ge(t2_evac, p)
                for h in range(HP):
                    mm = pe.transpose(b_st[0:ROWS, h // 4, (h % 4) * P:(h % 4) * P + ROWS],
                                      p2[p % 2][0:ROWS, 2 * h:2 * h + 2, :].rearrange("p a m -> p (a m)")[:, 0:ROWS],
                                      ident[0:ROWS, 0:ROWS])
                mm.then_inc(t2_ready, 1)

            def pv2(p):
                pe.wait_ge(t2_evac, p + 1)
                pe.wait_ge(c_evac, 8 + p + 1)
                if p > 0:
                    pe.wait_ge(z2_norm, p)
                for h in range(HP):
                    for r in range(2):
                        mm = pe.matmul(b_vo[0][SLOT * r:SLOT * r + S, h * 2 * XE:(h + 1) * 2 * XE],
                                       pT2[p % 2][0:ROWS, h, SLOT * r:SLOT * r + S], v2[0:ROWS, 2 * p + r, h, :],
                                       start=True, stop=True)
                mm.then_inc(pv2_ready, 1)

            def transposes3(p):
                pe.wait_ge(z2_norm, p + 1)
                if p > 0:
                    pe.wait_ge(z2_lo, p)
                for k in range(KD):
                    mm = pe.transpose(b_qk[0][:, k * D:k * D + ROWS], z2n[p % 2][0:ROWS, k * P:(k + 1) * P],
                                      ident[0:ROWS, 0:ROWS])
                mm.then_inc(z2_ready, 1)

            def out2(p, j):
                pe.wait_ge(z2_lo, p + 1)
                if j > 0:
                    pe.wait_ge(out2_added, j)
                for i, t in enumerate(o_tiles(j)):
                    cols = slice(t * P, (t + 1) * P)
                    mm = three(b_qk[1][:, i * D:(i + 1) * D],
                               [(tuple(z[:, k, cols] for z in z2), tuple(w[:, k, :] for w in wout))
                                for k in range(KD)])
                mm.then_inc(out2_ready, 1)

            def hidden(j):
                tiles = o_tiles(j)
                cols = slice(tiles.start * P, tiles.stop * P)
                pe.wait_ge(xT_lo, 4 + j + 1)
                for m in range(KD):
                    mm = three(b_vo[1][:, m * D:m * D + len(tiles) * P],
                               [(tuple(w[:, k, m * P:(m + 1) * P] for w in w1), tuple(x[:, k, cols] for x in x2))
                                for k in range(KD)])
                mm.then_inc(h_ready, 1)

            def ranks(t):
                if t >= 2:
                    pe.wait_ge(av_done, t - 1)
                three(b_z[:, t % 2, :], [(tuple(x[:, k, t * P:(t + 1) * P] for x in x2),
                                          tuple(w[:, k, :] for w in vw)) for k in range(KD)]).then_inc(vx_ready, 1)

            def logits(j):
                pe.wait_ge(h_evac, j + 1)
                for n in range(len(o_tiles(j))):
                    for k in range(KD):
                        mm = pe.matmul(b_vo[1][:, n * EXPERTS:(n + 1) * EXPERTS], hT[:, k, n * P:(n + 1) * P],
                                       w2_s[:, k, :], start=(k == 0), stop=(k == KD - 1))
                mm.then_inc(lg_ready, 1)

            def transpose_av(t):
                pe.wait_ge(av_done, t + 1)
                if t >= 2:
                    pe.wait_ge(avT_lo, t - 1)
                for c in range(KR):
                    mm = pe.transpose(avT_bank[t % 2][:, c, :], av[:, t % 2, c * P:(c + 1) * P], ident[:])
                mm.then_inc(avT_ready, 1)

            def experts(t):
                j, n = t // 2, t % 2
                if n == 0 and j >= 2:
                    pe.wait_ge(u_added, j - 1)
                pe.wait_ge(avT_lo, t + 1)
                mm = three(b_st[:, j % 2, n * D:(n + 1) * D],
                           [(tuple(a[n][:, c, :] for a in avT), tuple(w[:, c, :] for w in uw)) for c in range(KR)])
                if t + 1 == o_tiles(j).stop:
                    mm.then_inc(u_ready, 1)

            pe.wait_ge(w_lo[K_], (NG + 1) * G)
            pe.wait_ge(k2_dve, 8)
            pe.wait_ge(k2_pool, 8)
            for u in range(PAIRS + 4):
                if u < PAIRS:
                    scores2(u)
                if u < 2:
                    latent(14 + u)
                    queries(4 + 2 * u)
                    queries(5 + 2 * u)
                if 0 <= u - 1 < PAIRS:
                    transposes2(u - 1)
                if 0 <= u - 2 < PAIRS:
                    pv2(u - 2)
                if u == PAIRS:
                    hidden(0)
                if 0 <= u - 3 < PAIRS:
                    transposes3(u - 3)
                if u == PAIRS:
                    pe.wait_ge(sub2_done, PAIRS)
                    ranks(0)
                if u == PAIRS + 1:
                    logits(0)
                    ranks(1)
                    transpose_x(5)
                if u == PAIRS + 2:
                    pe.wait_ge(z2_norm, PAIRS)
                    pe.wait_ge(z2_lo, PAIRS)
                    transpose_av(0)
                    transpose_av(1)
                if 0 <= u - 4 and (j := out2_after(u - 4)) is not None:
                    out2(u - 4, j)
                if u == PAIRS - 1:
                    pe.wait_ge(w_lo[V_], 2 * NG + 2)
                    pe.wait_ge(w_lo[O_], 2 * NG + 2)
                    pe.wait_ge(d_small, 48)
                    transpose_x(4)
            pe.wait_ge(t2_evac, PAIRS)
            for j in range(1, 4):
                hidden(j)
                ranks(2 * j)
                experts(2 * j - 2)
                logits(j)
                if j < 3:
                    ranks(2 * j + 1)
                    transpose_x(5 + j)
                experts(2 * j - 1)
                for t in o_tiles(j):
                    transpose_av(t)
            experts(6)


def lay_out(inputs):
    import numpy as np
    a = {k: np.asarray(v) for k, v in inputs.items()}
    w = np.zeros((NG + 1, 4, P, W), np.float32)
    for m, name in ((Q_, "L0_attn_W_Q"), (K_, "L0_attn_W_K"), (V_, "L0_attn_W_V")):
        w[:NG, m] = a[name].reshape(NG, G, E, KD, P).transpose(0, 4, 3, 1, 2).reshape(NG, P, W)
    w[:NG, O_] = a["L0_attn_W_O"].reshape(NG, G, D, E).transpose(0, 3, 1, 2).reshape(NG, P, W)
    wq = a["L0_xattn_Wq"].reshape(NHG, 1, SLOT, KD, P).repeat(2, axis=1)
    w[NG, Q_] = wq.transpose(4, 3, 0, 1, 2).reshape(P, W)
    wo = a["L0_xattn_Wout"].reshape(D, KD, P).transpose(2, 1, 0)
    w1 = a["L0_ffn_W1"].reshape(KD, P, D).transpose(1, 0, 2)
    w[NG, K_] = np.concatenate([wo, w1], axis=2).reshape(P, W)
    w[NG, V_] = a["L0_ffn_V"].reshape(EXPERTS * RANK, KD, P).transpose(2, 1, 0).reshape(P, W)
    w[NG, O_] = a["L0_ffn_U"].transpose(0, 2, 1).reshape(KR, P, D).transpose(1, 0, 2).reshape(P, W)
    wk, wv = a["L0_xattn_Wkv_expand"].reshape(2, D, XL)
    return {
        "x": a["x"].reshape(N, D),
        "xT": a["x"].transpose(2, 0, 1),
        "weights": w,
        "ctxT": a["ctx_512"].transpose(2, 0, 1),
        "wk_dup": wk.reshape(NHG, 1, SLOT, XL).repeat(2, axis=1).transpose(3, 0, 1, 2).reshape(XL, NHG, P),
        "wv": wv.T,
        "w2": a["L0_ffn_W2"].reshape(KD, P, EXPERTS).transpose(1, 0, 2),
        "b1": a["L0_ffn_b1"].reshape(KD, P).T,
        "b2": a["L0_ffn_b2"],
    }


def kernel(**inputs):
    import numpy as np
    import concourse.bacc as bacc
    from concourse.bass_utils import run_bass_kernel_spmd

    nc = bacc.Bacc("TRN2", target_bir_lowering=False, num_devices=1)
    arrays = {n: np.ascontiguousarray(a) for n, a in lay_out(inputs).items()}
    aps = {n: nc.dram_tensor(n, a.shape, mybir.dt.from_np(a.dtype), kind="ExternalInput").ap()
           for n, a in arrays.items()}
    out = nc.dram_tensor("out", (N, D), F32, kind="ExternalOutput").ap()
    build(nc, out=out, **aps)
    r = run_bass_kernel_spmd(nc, [arrays], core_ids=[0])
    return r.results[0]["out"].reshape(NB, S, D)
```

```python
from contextlib import ExitStack

import concourse.bass as bass
from concourse import mybir

ALU = mybir.AluOpType
ACT = mybir.ActivationFunctionType
AX_X = mybir.AxisListType.X
F32 = mybir.dt.float32
F32R = mybir.dt.float32r
BF16 = mybir.dt.bfloat16

NB, S, D = 16, 56, 256
N = NB * S
P = 128
TILES = N // P
KD = D // P
NH, E = 16, 128
G = 4
NG = NH // G
SLOT = 64
ROWS = SLOT + S
PAIRS = NB // 2
HALF = N // 2
XH, XE, XL = 16, 16, 64
HG = 4
GP = XH // (2 * HG)
HP = XH // 2
EXPERTS, RANK = 8, 64
KR = EXPERTS * RANK // P
EPS = 1e-5
MASKED = -1e30
W = 4 * D
Q_, K_, V_, O_ = range(4)
WARM_UP = 10
ATTN_SCALE = float(E) ** -0.5
XATTN_SCALE = float(XE) ** -0.5


def build(nc, x, xT, weights, ctxT, wk, wv, w2, b1, b2, out):
    with ExitStack() as ctx:
        def sb(name, shape, dt=F32):
            return ctx.enter_context(nc.sbuf_tensor(name, shape, dt))

        def ps(name, shape):
            return ctx.enter_context(nc.psum_tensor(name, shape, F32))

        def sem(name):
            return ctx.enter_context(nc.semaphore(name))

        raw = sb("raw", [P, 4, W])
        w_h = sb("w_h", [P, 4, W], F32R)
        w_l = sb("w_l", [P, 4, W], F32R)
        xraw = sb("xraw", [P, KD, NB, S])
        xt_h = sb("xt_h", [P, KD, NB, SLOT], F32R)
        xt_l = sb("xt_l", [P, KD, NB, SLOT], F32R)
        qT = sb("qT", [P, N])
        kT = sb("kT", [P, N])
        v = sb("v", [P, PAIRS, G * E])
        prob = sb("prob", [P, 8, SLOT])
        probn = sb("probn", [P, 8, SLOT])
        pT = sb("pT", [P, PAIRS, 2 * S])
        mx = sb("mx", [P, 8])
        rs = sb("rs", [P, 8])
        rinv = sb("rinv", [P, 8])
        z_h = sb("z_h", [P, G, N], F32R)
        z_l = sb("z_l", [P, G, N], F32R)
        acc = sb("acc", [P, TILES, D])
        ident = sb("ident", [P, P])
        ident_b = sb("ident_b", [P, P], BF16)
        mask = sb("mask", [P, 8, SLOT], BF16)
        hmask = sb("hmask", [P, HG])
        still = sb("still", [P, 512], BF16)
        neg_half = sb("neg_half", [P, 2])
        ctx_raw = sb("ctx_raw", [P, 1 + NB, SLOT])
        ctx_hl = sb("ctx_hl", [P, 1 + NB, SLOT], F32R)
        wk_h = sb("wk_h", [P, GP, P], F32R)
        wk_l = sb("wk_l", [XL, GP, P], F32R)
        wv_h = sb("wv_h", [P, D], F32R)
        wv_l = sb("wv_l", [XL, D], F32R)
        k2 = sb("k2", [P, GP, 2, PAIRS, HG, S])
        v2 = sb("v2", [P, NB, HP, 2 * XE])

        w2_s = sb("w2_s", [P, KD, EXPERTS])
        b1_s = sb("b1_s", [P, KD])
        b2_s = sb("b2_s", [EXPERTS, 1])
        stats = sb("stats", [P, TILES, 6])
        mv = sb("mv", [P, TILES, 2])
        veps = sb("veps", [P, TILES])
        rstd = sb("rstd", [P, TILES])
        nmean = sb("nmean", [P, TILES])
        shift = sb("shift", [P, TILES])
        mx2 = sb("mx2", [P, 2, XH])
        rs2 = sb("rs2", [P, 2, XH])
        rinv2 = sb("rinv2", [P, 2, XH])
        hT = sb("hT", [P, KD, 2 * P])
        lgT = sb("lgT", [EXPERTS, 2 * P])
        lg = sb("lg", [P, 2, EXPERTS])
        lgm = sb("lgm", [P, 2])
        lgs = sb("lgs", [P, 2])
        lgr = sb("lgr", [P, 2])
        alpha = sb("alpha", [P, 2, EXPERTS])
        av = sb("av", [P, 2, EXPERTS * RANK])
        wk_raw = av[:, 0, 0:D].rearrange("p (g n) -> p g n", g=GP)
        wv_raw = av[:, 1, 0:D]

        def flat(t):
            return t[:].rearrange({3: "p a b -> p (a b)", 4: "p a b c -> p (a b c)"}[len(t.shape)])

        def halves(t, at):
            return flat(t)[:, at:at + KD * N].rearrange("p (k n) -> p k n", k=KD)

        x1 = [halves(t, 0) for t in (xt_h, xt_l)]
        z2 = [halves(t, 0) for t in (z_h, z_l)]
        x2 = [halves(t, KD * N) for t in (z_h, z_l)]
        q2 = flat(v)[:, 0:GP * 2 * PAIRS * ROWS].rearrange("p (g y a n) -> p g y a n", g=GP, y=2, a=PAIRS)
        p2 = [raw[:, i, :].rearrange("p (h m) -> p h m", m=SLOT) for i in (Q_, K_, O_)]
        pT2 = [flat(t)[:, at:at + HP * ROWS].rearrange("p (h n) -> p h n", h=HP)
               for t, at in ((raw, V_ * W), (xraw, 0))]
        avT = [[flat(t)[:, i * 512:(i + 1) * 512].rearrange("p (c n) -> p c n", c=KR) for i in range(2)]
               for t in (xt_h, xt_l)]
        wq2 = [t[:, Q_, :].rearrange("p (k n) -> p k n", k=KD) for t in (w_h, w_l)]
        wout = [t[:, K_, :].rearrange("p (k n) -> p k n", k=KD)[:, :, 0:D] for t in (w_h, w_l)]
        w1 = [t[:, K_, :].rearrange("p (k n) -> p k n", k=KD)[:, :, D:2 * D] for t in (w_h, w_l)]
        vw = [t[:, V_, :].rearrange("p (k n) -> p k n", k=KD) for t in (w_h, w_l)]
        uw = [t[:, O_, :].rearrange("p (c n) -> p c n", c=KR) for t in (w_h, w_l)]

        b_qk = [ps(f"b_qk{i}", [P, 512]) for i in range(2)]
        b_st = ps("b_st", [P, 2, 512])
        b_s = b_st[:, 0, :]
        b_t = b_st[:, 1, :]
        b_z = ps("b_z", [P, 2, 512])
        b_vo = [ps(f"b_vo{i}", [P, 512]) for i in range(2)]

        z2_bank = b_vo[0][:, 0:2 * 2 * S].rearrange("p (k n) -> p k n", k=KD)
        avT_bank = [b[:].rearrange("p (c n) -> p c n", c=KR) for b in (b_qk[0], b_vo[0])]

        d_x, d_ctx, d_small = sem("d_x"), sem("d_ctx"), sem("d_small")
        d_xT = [sem(f"d_xT{c}") for c in range(2)]
        d_first = [sem(f"d_first{m}") for m in (Q_, K_)]
        d_w = [sem(f"d_w{m}") for m in range(4)]
        zeroed, consts, still_zero = sem("zeroed"), sem("consts"), sem("still_zero")
        x_hi_act, x_hi_dve, x_lo = sem("x_hi_act"), sem("x_hi_dve"), sem("x_lo")
        w_hi = [sem(f"w_hi{m}") for m in range(4)]
        w_lo = [sem(f"w_lo{m}") for m in range(4)]
        qk_ready, qk_evac = sem("qk_ready"), sem("qk_evac")
        s_ready, max_done, sub_done = sem("s_ready"), sem("max_done"), sem("sub_done")
        exp_done, sum_done, recip_done, pn_ready = (
            sem("exp_done"), sem("sum_done"), sem("recip_done"), sem("pn_ready"))
        t_ready, pt_act, pt_dve = sem("t_ready"), sem("pt_act"), sem("pt_dve")
        z_ready, z_hi, z_lo = sem("z_ready"), sem("z_hi"), sem("z_lo")
        v_ready, v_evac = sem("v_ready"), sem("v_evac")
        o_ready, o_added = sem("o_ready"), sem("o_added")
        ctx_hi, ctx_lo = sem("ctx_hi"), sem("ctx_lo")
        keys_ready, keys_staged, k2_dve, k2_pool = (
            sem("keys_ready"), sem("keys_staged"), sem("k2_dve"), sem("k2_pool"))
        values_ready, values_placed = sem("values_ready"), sem("values_placed")
        bn_done, aggr_done, ve_ready, rstd_ready = (
            sem("bn_done"), sem("aggr_done"), sem("ve_ready"), sem("rstd_ready"))
        ln_dve, ln_act = sem("ln_dve"), sem("ln_act")
        nmean_ready, shift_ready = sem("nmean_ready"), sem("shift_ready")
        xT_ready, xT_hi, xT_lo = sem("xT_ready"), sem("xT_hi"), sem("xT_lo")
        q2_zeroed, p2_zeroed = sem("q2_zeroed"), sem("p2_zeroed")
        q2_ready, q2_act, q2_dve = sem("q2_ready"), sem("q2_act"), sem("q2_dve")
        s2_ready, max2_done, sub2_done, exp2_done, sum2_done, recip2_done = (
            sem("s2_ready"), sem("max2_done"), sem("sub2_done"), sem("exp2_done"), sem("sum2_done"),
            sem("recip2_done"))
        pn2_ready, t2_ready, t2_evac = sem("pn2_ready"), sem("t2_ready"), sem("t2_evac")
        z2_ready, z2_hi, z2_lo = sem("z2_ready"), sem("z2_hi"), sem("z2_lo")
        out2_ready, out2_added = sem("out2_ready"), sem("out2_added")
        lgT_ready, lgT_evac = sem("lgT_ready"), sem("lgT_evac")
        h_ready, h_evac, lg_ready, lg_step, lg_exp, alpha_done = (
            sem("h_ready"), sem("h_evac"), sem("lg_ready"), sem("lg_step"), sem("lg_exp"), sem("alpha_done"))
        vx_ready, av_done, avT_ready, avT_hi, avT_lo = (
            sem("vx_ready"), sem("av_done"), sem("avT_ready"), sem("avT_hi"), sem("avT_lo"))
        u_ready, u_added, stored = sem("u_ready"), sem("u_added"), sem("stored")

        def qk_cols(m, i):
            i = i if isinstance(i, slice) else slice(i, i + 1)
            return lambda t: t[:, m, :].rearrange("p (k n) -> p k n", k=KD)[:, :, i.start * E:i.stop * E]

        def half(m, i):
            return lambda t: t[:, m, i * W // 2:(i + 1) * W // 2]

        def w_landed(m, g):
            return (g + 1) * 16

        def ctx_uses(i):
            return (range(0), range(0, 2), range(2, 3), range(3, 4))[i]

        def out2_after(p):
            return {2: 0, 4: 1, 6: 2, 7: 3}.get(p)

        def staged(n):
            return flat(xraw)[:, n * HALF:(n + 1) * HALF]

        def key_blocks(n, rows, r):
            keys = staged(n)[SLOT * rows:SLOT * (rows + 1)].rearrange("p (a r m) -> p a r m", r=2, m=S)[:, :, r, :]
            return keys.unsqueeze(2).broadcast_to([SLOT, 4, HG, S])

        def head_blocks(r):
            return hmask[SLOT * r:SLOT * (r + 1), :].unsqueeze(1).unsqueeze(3).broadcast_to([SLOT, 4, HG, S])

        def value_bank(n):
            return (b_qk[0][:], b_qk[1][:], b_z[:, 0, :], b_z[:, 1, :], b_z[:, 0, :], b_vo[1][:], b_vo[1][:],
                    b_qk[0][:])[n]

        def xT_bank(n):
            return (b_st[:, n % 2, :] if n < 4 else b_vo[1][:]).rearrange("p (k n) -> p k n", k=KD)

        def on_act(layer, j):
            return layer == 1 or (layer, j) in ((0, 0), (2, 0), (2, 1), (2, 2))

        def acts_before(n):
            return sum(on_act(i // 4, i % 4) for i in range(n))

        def normalized(n):
            return (ln_act, acts_before(n) + 1) if on_act(n // 4, n % 4) else (ln_dve, n - acts_before(n) + 1)

        def o_tiles(j):
            return range(2 * j, min(2 * j + 2, TILES))

        block = ctx.enter_context(nc.Block())

        @block.sync
        def _(sp):
            first = [qk_cols(m, slice(0, 1))(raw) for m in (Q_, K_)]
            rest = [qk_cols(m, slice(1, G))(raw) for m in (Q_, K_)]
            cols = [weights[0, m].rearrange("p (k n) -> p k n", k=KD) for m in (Q_, K_)]
            xT_k = xT.rearrange("(k p) b s -> p k b s", p=P)
            sp.dma_start(first[Q_], cols[Q_][:, :, 0:E]).then_inc(d_first[Q_], 16)
            sp.dma_start(xraw[:, :, 0:NB // 2, :], xT_k[:, :, 0:NB // 2, :]).then_inc(d_xT[0], 16)
            sp.dma_start(first[K_], cols[K_][:, :, 0:E]).then_inc(d_first[K_], 16)
            sp.dma_start(xraw[:, :, NB // 2:, :], xT_k[:, :, NB // 2:, :]).then_inc(d_xT[1], 16)
            sp.dma_start(raw[:, V_, :], weights[0, V_]).then_inc(d_w[V_], 16)
            for m in (Q_, K_):
                sp.dma_start(rest[m], cols[m][:, :, E:G * E]).then_inc(d_w[m], 16)
            for r in range(2):
                sp.dma_start(ctx_raw[r * XL:(r + 1) * XL, :, 0:S], ctxT).then_inc(d_ctx, 16)
            sp.dma_start(wk_raw, wk).then_inc(d_ctx, 16)
            sp.dma_start(wv_raw, wv).then_inc(d_ctx, 16)
            sp.dma_start(acc[:], x.rearrange("(t p) d -> p t d", p=P)).then_inc(d_x, 16)
            sp.dma_start(raw[:, O_, :], weights[0, O_]).then_inc(d_w[O_], 16)
            sp.dma_start(w2_s[:], w2).then_inc(d_small, 16)
            sp.dma_start(b1_s[:], b1).then_inc(d_small, 16)
            sp.dma_start(b2_s[:], b2).then_inc(d_small, 16)
            with sp.Fori(1, NG + 1) as g:
                for m in range(4):
                    units = G if m in (Q_, K_) else 2
                    sp.wait_ge(w_hi[m], g * units)
                    sp.wait_ge(w_lo[m], g * units)
                    sp.dma_start(raw[:, m, :], weights[g, m]).then_inc(d_w[m], 16)
            for j in range(4):
                t = o_tiles(j)
                sp.wait_ge(*normalized(8 + j))
                sp.dma_start(out[t.start * P:t.stop * P].rearrange("(t p) d -> p t d", p=P),
                             acc[:, t.start:t.stop, :]).then_inc(stored, 16)
            sp.wait_ge(stored, 64)

        @block.gpsimd
        def _(pool):
            for t in (xt_h, xt_l):
                pool.memset(t[:, :, :, S:SLOT].bitcast(F32), 0.0).then_inc(zeroed, 1)
            pool.memset(ident[:], 0.0).then_inc(consts, 1)
            pool.memset(mask[:], 0.0).then_inc(consts, 1)
            pool.memset(probn[:], 0.0).then_inc(consts, 1)
            pool.memset(pT[:], 0.0).then_inc(zeroed, 1)
            pool.wait_ge(consts, 3)
            pool.affine_select(out=ident[:], in_=ident[:], compare_op=ALU.not_equal, fill=1.0, base=0,
                               pattern=[[-1, P]], channel_multiplier=1).then_inc(consts, 1)
            for r in range(2):
                pool.wait_ge(consts, 4 + r)
                rows = mask[SLOT * r:SLOT * (r + 1)]
                pool.affine_select(out=rows, in_=rows, compare_op=ALU.is_ge, fill=MASKED, base=0,
                                   pattern=[[0, 8], [-1, SLOT]], channel_multiplier=1).then_inc(consts, 1)
            pool.wait_ge(consts, 6)
            pool.tensor_copy(ident_b[:], ident[:]).then_inc(consts, 1)

            pool.memset(neg_half[:], -0.5).then_inc(consts, 1)
            pool.memset(ctx_raw[:, :, S:SLOT], 0.0).then_inc(consts, 1)
            pool.memset(hmask[:], 1.0).then_inc(consts, 1)
            for r in range(2):
                rows = hmask[SLOT * r:SLOT * (r + 1)]
                pool.wait_ge(consts, 10 + 2 * r)
                pool.affine_select(out=rows, in_=rows, compare_op=ALU.is_ge, fill=0.0, base=0,
                                   pattern=[[-XE, HG]], channel_multiplier=1).then_inc(consts, 1)
                pool.wait_ge(consts, 11 + 2 * r)
                pool.affine_select(out=rows, in_=rows, compare_op=ALU.is_ge, fill=0.0, base=XE - 1,
                                   pattern=[[XE, HG]], channel_multiplier=-1).then_inc(consts, 1)
            pool.wait_ge(consts, 14)
            pool.memset(v2[:], 0.0).then_inc(consts, 1)

            def norm(s, first=False):
                pool.wait_ge(recip_done, s + 1)
                if not first:
                    pool.wait_ge(t_ready, s)
                pool.tensor_tensor(probn[0:ROWS, :, 0:S], prob[0:ROWS, :, 0:S],
                                   rinv[0:ROWS, :].unsqueeze(2).broadcast_to([ROWS, 8, S]),
                                   ALU.mult).then_inc(pn_ready, 1)

            def split_lo(m, cols, count):
                pool.wait_ge(w_hi[m], count)
                pool.tensor_tensor(cols(w_l), cols(raw), cols(w_h).bitcast(F32), ALU.subtract).then_inc(w_lo[m], 1)

            def expand_keys(n):
                pool.wait_ge(keys_staged, n + 1)
                g, c = n % GP, n // GP
                for r in range(2):
                    pool.tensor_tensor(k2[0:SLOT, g, r, 4 * c:4 * c + 4, :, :],
                                       key_blocks(n, 0, r), head_blocks(0), ALU.mult).then_inc(k2_pool, 1)

            def group(g, first=False):
                for i in range(G):
                    s = g * G + i
                    if i > 0 or not first:
                        for m in (Q_, K_):
                            pool.wait_ge(qk_ready, s * 4)
                            split_lo(m, qk_cols(m, (i - 1) % G), s + G)
                    if first:
                        norm(s, i == 0)
                    if i == 2:
                        pool.wait_ge(v_ready, (g + 1) * PAIRS)
                        for h in range(2):
                            split_lo(V_, half(V_, h), (g + 1) * 2 + h + 1)
                    if i == 3:
                        if not first:
                            pool.wait_ge(o_ready, g * 4)
                        for h in range(2):
                            split_lo(O_, half(O_, h), g * 2 + h + 1)
                    if first:
                        for n in ctx_uses(i):
                            expand_keys(n)
                    else:
                        norm(s)

            group(0, first=True)
            with pool.Fori(1, NG) as g:
                group(g)
            for m in (Q_, K_):
                split_lo(m, qk_cols(m, G - 1), (NG + 1) * G)
            pool.wait_ge(z_ready, 2 * NH)
            pool.memset(q2, 0.0).then_inc(q2_zeroed, 1)

            def inverse_deviation(n):
                t = o_tiles(n % 4)
                pool.wait_ge(ve_ready, n + 1)
                pool.tensor_tensor(rstd[:, t.start:t.stop], veps[:, t.start:t.stop], neg_half[:, 0:len(t)],
                                   ALU.pow).then_inc(rstd_ready, 1)
                if on_act(n // 4, n % 4):
                    cols = slice(t.start, t.stop)
                    pool.wait_ge(rstd_ready, n + 1)
                    pool.wait_ge(nmean_ready, acts_before(n) + 1)
                    pool.tensor_tensor(shift[:, cols], nmean[:, cols], rstd[:, cols], ALU.mult).then_inc(shift_ready, 1)

            inverse_deviation(0)
            inverse_deviation(1)
            for m in (Q_, K_):
                pool.wait_ge(w_lo[m], (NG + 1) * G)
            for t in p2[0:2]:
                pool.memset(t[:, :, S:SLOT], 0.0).then_inc(p2_zeroed, 1)
            inverse_deviation(2)
            inverse_deviation(3)

            def norm2(p):
                pool.wait_ge(recip2_done, p + 1)
                rows = p2[p % 3][0:ROWS, :, 0:S]
                pool.tensor_tensor(rows, rows, rinv2[0:ROWS, p % 2, :].unsqueeze(2).broadcast_to([ROWS, XH, S]),
                                   ALU.mult).then_inc(pn2_ready, 1)

            split_lo(O_, half(O_, 0), NG * 2 + 1)
            split_lo(O_, half(O_, 1), NG * 2 + 2)
            pool.wait_ge(w_lo[O_], NG * 2 + 2)
            pool.memset(p2[2][:, :, S:SLOT], 0.0).then_inc(p2_zeroed, 1)
            for p in range(PAIRS):
                norm2(p)
                if p == 5:
                    inverse_deviation(4)
            for n in range(5, 12):
                inverse_deviation(n)

        @block.scalar
        def _(act):
            def split_first(m):
                act.wait_ge(d_first[m], 16)
                cols = qk_cols(m, 0)
                act.copy(cols(w_h), cols(raw)).then_inc(w_hi[m], 1)

            def split_hi(m, cols, landed):
                act.wait_ge(d_w[m], landed)
                act.copy(cols(w_h), cols(raw)).then_inc(w_hi[m], 1)

            split_first(Q_)
            for c in range(2):
                act.wait_ge(d_xT[c], 16)
                b = slice(c * NB // 2, (c + 1) * NB // 2)
                act.copy(xt_h[:, 0, b, 0:S], xraw[:, 0, b]).then_inc(x_hi_act, 1)
                if c == 0:
                    split_first(K_)

            def evac_qk(s, n):
                act.wait_ge(qk_ready, s * 4 + n + 1)
                dst = (qT, kT)[n % 2]
                act.copy(dst[:, (n // 2) * HALF:(n // 2 + 1) * HALF], b_qk[n % 2][:, 0:HALF]).then_inc(qk_evac, 1)

            def evac_pT(s):
                act.wait_ge(t_ready, s + 1)
                act.copy(pT[0:S, :, 0:S],
                         b_t[0:S, :].rearrange("p (a m) -> p a m", m=SLOT)[:, :, 0:S]).then_inc(pt_act, 1)

            def exp(s):
                act.wait_ge(sub_done, s + 1)
                act.activation(prob[0:ROWS, :, 0:S], prob[0:ROWS, :, 0:S], ACT.Exp,
                               scale=ATTN_SCALE).then_inc(exp_done, 1)

            def evac_z_hi(s, i):
                for c in range(2):
                    act.wait_ge(z_ready, s * 2 + c + 1)
                    act.copy(z_h[:, i, c * HALF:(c + 1) * HALF], b_z[:, c, 0:HALF]).then_inc(z_hi, 1)

            def stage_keys(n):
                act.wait_ge(keys_ready, n + 1)
                act.wait_ge(x_lo, 4)
                act.copy(staged(n), b_vo[n % 2][:, 0:HALF]).then_inc(keys_staged, 1)

            def place_values(n):
                act.wait_ge(values_ready, n + 1)
                b = 2 * n
                parts = ((0, 0, 2, b - 1), (1, 0, 2, b)) if n > 0 else ((0, 0, 1, NB - 1), (0, 1, 2, 0), (1, 0, 2, 0))
                for r, start, stop, dst in parts:
                    src = value_bank(n)[SLOT * r:SLOT * r + S, :].rearrange("p (b h r e) -> p b h r e", b=2, h=HP, r=2)
                    ins = act.copy(v2[SLOT * r:SLOT * r + S, dst:dst + stop - start, :, r * XE:(r + 1) * XE],
                                   src[:, start:stop, :, r, :])
                ins.then_inc(values_placed, 1)

            def group(g, first=False):
                for i in range(G):
                    s = g * G + i
                    begin = first and i == 0
                    if not begin:
                        act.wait_ge(s_ready, s)
                    for n in range(4):
                        evac_qk(s, n)
                        if begin and n in (1, 2):
                            split_hi(V_, half(V_, n - 1), w_landed(V_, 0))
                        if n < 2 and not (first and i <= 1):
                            split_hi(n, qk_cols(n, (i - 1) % G), w_landed(n, g if i == 0 else g + 1))
                        if n == 2 and i == 2:
                            act.wait_ge(v_ready, (g + 1) * PAIRS)
                            split_hi(V_, half(V_, 0), w_landed(V_, g + 1))
                        if n == 2 and i == 3:
                            if not first:
                                act.wait_ge(o_ready, g * 4)
                            split_hi(O_, half(O_, 0), w_landed(O_, g))
                        if first and n in (1, 3) and n // 2 < len(ctx_uses(i)):
                            stage_keys(ctx_uses(i)[n // 2])
                    if begin:
                        for m in (Q_, K_):
                            split_hi(m, qk_cols(m, 1), w_landed(m, 0))
                    else:
                        evac_pT(s - 1)
                    if i == 2:
                        split_hi(V_, half(V_, 1), w_landed(V_, g + 1))
                    if i == 3:
                        split_hi(O_, half(O_, 1), w_landed(O_, g))
                    exp(s)
                    if not begin:
                        evac_z_hi(s - 1, (i - 1) % G)
                    if i == 0:
                        for j in range(PAIRS):
                            act.wait_ge(v_ready, g * PAIRS + j + 1)
                            act.copy(v[0:ROWS, j, :], b_vo[j % 2][0:ROWS, :]).then_inc(v_evac, 1)
                            if first and j in (0, 1):
                                for m in (Q_, K_):
                                    split_hi(m, qk_cols(m, 2 + j), w_landed(m, 0))
                            if first and j == 3:
                                act.wait_ge(d_ctx, 64)
                                act.wait_ge(consts, 9)
                                act.copy(ctx_hl[:], ctx_raw[:]).then_inc(ctx_hi, 1)
                            if first and j == 4:
                                act.copy(wk_h[:], wk_raw).then_inc(ctx_hi, 1)
                                act.copy(wv_h[:], wv_raw).then_inc(ctx_hi, 1)
                    if first and i == 1:
                        for m in (Q_, K_):
                            split_hi(m, qk_cols(m, 0), w_landed(m, 1))
            group(0, first=True)
            with act.Fori(1, NG) as g:
                group(g)
            for m in (Q_, K_):
                split_hi(m, qk_cols(m, G - 1), w_landed(m, NG))
            evac_pT(NH - 1)
            place_values(0)
            evac_z_hi(NH - 1, G - 1)

            def evac_xT(n, dst):
                t = o_tiles(n % 4)
                act.wait_ge(xT_ready, n + 1)
                act.copy(dst[0][:, :, t.start * P:t.stop * P], xT_bank(n)[:, :, 0:len(t) * P]).then_inc(xT_hi, 1)

            def normalize(n):
                act.wait_ge(shift_ready, acts_before(n) + 1)
                for t in o_tiles(n % 4):
                    ins = act.activation(acc[:, t, :], acc[:, t, :], ACT.Identity, bias=shift[:, t:t + 1],
                                         scale=rstd[:, t:t + 1])
                ins.then_inc(ln_act, 1)

            def evac_q2(n):
                g, c = n % GP, n // GP
                act.wait_ge(q2_ready, n + 1)
                for odd in range(1 if n < 2 else 2):
                    rows = slice(SLOT * odd, SLOT * (odd + 1))
                    src = b_qk[n % 2][rows, 0:HALF].rearrange("p (a r m) -> p a r m", r=2, m=S)
                    for r in range(2):
                        ins = act.copy(q2[rows, g, r ^ odd, 4 * c:4 * c + 4, SLOT * r:SLOT * r + S], src[:, :, r, :])
                ins.then_inc(q2_act, 1)

            place_values(1)
            place_values(2)
            normalize(0)
            evac_xT(0, x1)
            evac_xT(1, x1)
            place_values(3)
            place_values(4)
            act.wait_ge(q2_zeroed, 1)
            evac_q2(0)
            evac_q2(1)
            evac_xT(2, x1)
            evac_xT(3, x1)
            for h in range(2):
                split_hi(O_, half(O_, h), w_landed(O_, NG))

            def relu(j):
                cols = len(o_tiles(j)) * P
                act.wait_ge(h_ready, j + 1)
                for m in range(KD):
                    ins = act.activation(hT[:, m, 0:cols], b_vo[1][:, m * D:m * D + cols], ACT.Relu,
                                         bias=b1_s[:, m:m + 1])
                ins.then_inc(h_evac, 1)

            def evac_logits(j):
                act.wait_ge(lgT_ready, j + 1)
                cols = slice(0, len(o_tiles(j)) * P)
                act.activation(lgT[:, cols], b_vo[1][0:EXPERTS, cols], ACT.Identity, bias=b2_s[:, 0:1]
                               ).then_inc(lgT_evac, 1)

            def logits_exp(j):
                nt = len(o_tiles(j))
                act.wait_ge(lg_step, 2 * j + 2)
                act.activation(lg[:, 0:nt, :], lg[:, 0:nt, :], ACT.Exp).then_inc(lg_exp, 1)

            def evac_avT(t):
                act.wait_ge(avT_ready, t + 1)
                act.copy(avT[0][t % 2], avT_bank[t % 2]).then_inc(avT_hi, 1)

            def evac_pT2(p):
                act.wait_ge(t2_ready, p + 1)
                if p >= 2:
                    act.wait_ge(z2_ready, p - 1)
                act.copy(pT2[p % 2][0:ROWS, :, :],
                         b_st[0:ROWS, :, :].rearrange("p a (h n) -> p (a h) n", n=P)[:, :, 0:ROWS]
                         ).then_inc(t2_evac, 1)

            def evac_z2_hi(p):
                act.wait_ge(z2_ready, p + 1)
                act.copy(z2[0][:, :, p * 2 * S:(p + 1) * 2 * S], z2_bank).then_inc(z2_hi, 1)

            def exp2(p):
                act.wait_ge(sub2_done, 2 * p + 2)
                act.activation(p2[p % 3][0:ROWS, :, 0:S], p2[p % 3][0:ROWS, :, 0:S], ACT.Exp,
                               scale=XATTN_SCALE).then_inc(exp2_done, 1)

            for u in range(PAIRS):
                if u >= 3:
                    evac_pT2(u - 3)
                    evac_z2_hi(u - 3)
                if u == PAIRS - 1:
                    normalize(4)
                    evac_pT2(5)
                exp2(u)
                if u < 2:
                    evac_q2(2 + u)
                if u == 1:
                    place_values(5)
                if u == 2:
                    place_values(6)
            act.wait_ge(d_small, 48)
            evac_xT(4, x2)
            place_values(7)
            evac_z2_hi(5)
            relu(0)
            evac_pT2(6)
            normalize(5)
            evac_logits(0)
            evac_pT2(7)
            logits_exp(0)
            evac_z2_hi(6)
            evac_xT(5, x2)
            evac_avT(0)
            evac_z2_hi(7)
            relu(1)
            normalize(6)
            evac_avT(1)
            normalize(7)
            evac_logits(1)
            logits_exp(1)
            evac_xT(6, x2)
            evac_avT(2)
            evac_avT(3)
            relu(2)
            evac_logits(2)
            logits_exp(2)
            evac_xT(7, x2)
            normalize(8)
            relu(3)
            evac_avT(4)
            evac_logits(3)
            evac_avT(5)
            logits_exp(3)
            normalize(9)
            evac_avT(6)
            normalize(10)

        @block.vector
        def _(dve):
            def split_lo(m, cols, count):
                dve.wait_ge(w_hi[m], count)
                dve.tensor_tensor(cols(w_l), cols(raw), cols(w_h).bitcast(F32), ALU.subtract).then_inc(w_lo[m], 1)

            def batches(c):
                return slice(c * NB // 2, (c + 1) * NB // 2)

            def split_x_hi(c):
                dve.wait_ge(d_xT[c], 16)
                dve.tensor_copy(xt_h[:, 1, batches(c), 0:S], xraw[:, 1, batches(c)]).then_inc(x_hi_dve, 1)

            def split_x_lo(c):
                for k, done in ((0, x_hi_act), (1, x_hi_dve)):
                    dve.wait_ge(done, c + 1)
                    dve.tensor_tensor(xt_l[:, k, batches(c), 0:S], xraw[:, k, batches(c)],
                                      xt_h[:, k, batches(c), 0:S].bitcast(F32), ALU.subtract).then_inc(x_lo, 1)

            dve.memset(still[:], 0.0).then_inc(still_zero, 1)
            split_lo(Q_, qk_cols(Q_, 0), 1)
            split_x_hi(0)
            split_x_lo(0)
            split_lo(K_, qk_cols(K_, 0), 1)
            split_x_hi(1)
            split_x_lo(1)
            for h in range(2):
                split_lo(V_, half(V_, h), h + 1)
            for m in (Q_, K_):
                split_lo(m, qk_cols(m, 1), 2)

            def evac_pT(s):
                dve.wait_ge(t_ready, s + 1)
                dve.tensor_copy(pT[SLOT:ROWS, :, S:2 * S],
                                b_t[SLOT:ROWS, :].rearrange("p (a m) -> p a m", m=SLOT)[:, :, 0:S]).then_inc(pt_dve, 1)

            def center(s, first=False):
                dve.wait_ge(s_ready, s + 1)
                scores = b_s[0:ROWS, :].rearrange("p (a m) -> p a m", m=SLOT)[:, :, 0:S]
                dve.tensor_reduce(mx[0:ROWS, :], scores, AX_X, ALU.max).then_inc(max_done, 1)
                dve.wait_ge(max_done, s + 1)
                if not first:
                    dve.wait_ge(pn_ready, s)
                dve.tensor_tensor(prob[0:ROWS, :, 0:S], scores,
                                  mx[0:ROWS, :].unsqueeze(2).broadcast_to([ROWS, 8, S]),
                                  ALU.subtract).then_inc(sub_done, 1)

            def row_sums(s):
                dve.wait_ge(exp_done, s + 1)
                dve.tensor_reduce(rs[0:ROWS, :], prob[0:ROWS, :, 0:S], AX_X, ALU.add).then_inc(sum_done, 1)
                dve.wait_ge(sum_done, s + 1)
                dve.reciprocal(rinv[0:ROWS, :], rs[0:ROWS, :]).then_inc(recip_done, 1)

            def evac_z_lo(s, i):
                for c in range(2):
                    dve.wait_ge(z_hi, s * 2 + c + 1)
                    cols = slice(c * HALF, (c + 1) * HALF)
                    dve.tensor_tensor(z_l[:, i, cols], b_z[:, c, 0:HALF], z_h[:, i, cols].bitcast(F32),
                                      ALU.subtract).then_inc(z_lo, 1)

            def add_o_step(g, j):
                dve.wait_ge(o_ready, g * 4 + j + 1)
                t = o_tiles(j)
                a = acc[:, t.start:t.stop, :]
                dve.tensor_tensor(a, b_vo[j % 2][:, 0:len(t) * D].rearrange("p (t d) -> p t d", d=D), a,
                                  ALU.add).then_inc(o_added, 1)

            def add_o(g):
                for j in range(4):
                    add_o_step(g, j)

            def expand_keys(n):
                g, c = n % GP, n // GP
                dve.wait_ge(keys_staged, n + 1)
                for r in range(2):
                    dve.tensor_tensor(k2[SLOT:P, g, 1 - r, 4 * c:4 * c + 4, :, :],
                                      key_blocks(n, 1, r), head_blocks(1), ALU.mult).then_inc(k2_dve, 1)

            def group(g, first=False):
                for i in range(G):
                    s = g * G + i
                    begin = first and i == 0
                    if not begin:
                        evac_pT(s - 1)
                    center(s, begin)
                    row_sums(s)
                    if not begin:
                        evac_z_lo(s - 1, (i - 1) % G)
                    if begin:
                        for h in range(2, G):
                            for m in (Q_, K_):
                                split_lo(m, qk_cols(m, h), h + 1)
                        for n, (lo, hi, src, rows) in enumerate((
                                (ctx_hl, ctx_hl, ctx_raw, slice(XL, 2 * XL)),
                                (wk_l, wk_h, wk_raw, slice(0, XL)), (wv_l, wv_h, wv_raw, slice(0, XL)))):
                            dve.wait_ge(ctx_hi, n + 1)
                            dve.tensor_tensor(lo[rows], src[rows], hi[rows].bitcast(F32),
                                              ALU.subtract).then_inc(ctx_lo, 1)
                    if first:
                        if i == 1:
                            dve.wait_ge(consts, 14)
                        for n in ctx_uses(i):
                            expand_keys(n)
                    if i == 0 and not first:
                        add_o(g - 1)

            dve.wait_ge(zeroed, 3)
            group(0, first=True)
            dve.wait_ge(d_x, 16)
            with dve.Fori(1, NG) as g:
                group(g)
            evac_pT(NH - 1)
            evac_z_lo(NH - 1, G - 1)

            def moments(layer, j, added):
                sem_, count = added
                tiles = o_tiles(j)
                dve.wait_ge(sem_, count)
                for t in tiles:
                    dve.bn_stats(stats[:, t, :], acc[:, t, :]).then_inc(bn_done, 1)
                for t in tiles:
                    dve.wait_ge(bn_done, layer * TILES + t + 1)
                    dve.bn_aggr(mv[:, t, :], stats[:, t, :]).then_inc(aggr_done, 1)
                dve.wait_ge(aggr_done, layer * TILES + tiles.stop)
                dve.tensor_scalar(veps[:, tiles.start:tiles.stop], mv[:, tiles.start:tiles.stop, 1], EPS, None,
                                  ALU.add).then_inc(ve_ready, 1)
                if on_act(layer, j):
                    dve.tensor_scalar(nmean[:, tiles.start:tiles.stop], mv[:, tiles.start:tiles.stop, 0], -1.0,
                                      None, ALU.mult).then_inc(nmean_ready, 1)

            def normalize(layer, j):
                dve.wait_ge(rstd_ready, layer * 4 + j + 1)
                for t in o_tiles(j):
                    ins = dve.tensor_scalar(acc[:, t, :], acc[:, t, :], mv[:, t, 0:1], rstd[:, t:t + 1],
                                            ALU.subtract, ALU.mult)
                ins.then_inc(ln_dve, 1)

            def evac_xT(n, dst):
                t = o_tiles(n % 4)
                cols = slice(t.start * P, t.stop * P)
                dve.wait_ge(xT_hi, n + 1)
                dve.tensor_tensor(dst[1][:, :, cols], xT_bank(n)[:, :, 0:len(t) * P],
                                  dst[0][:, :, cols].bitcast(F32), ALU.subtract).then_inc(xT_lo, 1)

            def evac_q2(n):
                g, c = n % GP, n // GP
                dve.wait_ge(q2_ready, n + 1)
                src = b_qk[n % 2][SLOT:P, 0:HALF].rearrange("p (a r m) -> p a r m", r=2, m=S)
                for r in range(2):
                    ins = dve.tensor_copy(q2[SLOT:P, g, 1 - r, 4 * c:4 * c + 4, SLOT * r:SLOT * r + S], src[:, :, r, :])
                ins.then_inc(q2_dve, 1)

            def first_norm(j):
                add_o_step(NG - 1, j)
                moments(0, j, (o_added, NG * 4 - 4 + j + 1))

            dve.wait_ge(o_added, NG * 4 - 4)
            first_norm(0)
            first_norm(1)
            add_o_step(NG - 1, 2)
            normalize(0, 1)
            evac_xT(0, x1)
            moments(0, 2, (o_added, NG * 4 - 1))
            evac_xT(1, x1)
            normalize(0, 2)
            first_norm(3)
            dve.wait_ge(q2_zeroed, 1)
            evac_q2(0)
            normalize(0, 3)
            evac_q2(1)
            evac_xT(2, x1)
            evac_xT(3, x1)

            def experts_out(j):
                t = o_tiles(j)
                a = acc[:, t.start:t.stop, :]
                dve.wait_ge(u_ready, j + 1)
                dve.tensor_tensor(a, b_st[:, j % 2, 0:len(t) * D].rearrange("p (t d) -> p t d", d=D), a,
                                  ALU.add).then_inc(u_added, 1)
                moments(2, j, (u_added, j + 1))

            def softmax(j):
                nt = len(o_tiles(j))
                dve.wait_ge(lg_ready, j + 1)
                logits = b_vo[1][:, 2 * P:2 * P + nt * EXPERTS].rearrange("p (t e) -> p t e", e=EXPERTS)
                dve.tensor_reduce(lgm[:, 0:nt], logits, AX_X, ALU.max).then_inc(lg_step, 1)
                dve.wait_ge(lg_step, 2 * j + 1)
                dve.tensor_tensor(lg[:, 0:nt, :], logits,
                                  lgm[:, 0:nt].unsqueeze(2).broadcast_to([P, nt, EXPERTS]),
                                  ALU.subtract).then_inc(lg_step, 1)
                dve.wait_ge(lg_exp, j + 1)
                dve.tensor_reduce(lgs[:, 0:nt], lg[:, 0:nt, :], AX_X, ALU.add).then_inc(alpha_done, 1)
                dve.wait_ge(alpha_done, 3 * j + 1)
                dve.reciprocal(lgr[:, 0:nt], lgs[:, 0:nt]).then_inc(alpha_done, 1)
                dve.wait_ge(alpha_done, 3 * j + 2)
                dve.tensor_tensor(alpha[:, 0:nt, :], lg[:, 0:nt, :],
                                  lgr[:, 0:nt].unsqueeze(2).broadcast_to([P, nt, EXPERTS]),
                                  ALU.mult).then_inc(alpha_done, 1)

            def weigh(j):
                dve.wait_ge(alpha_done, 3 * j + 3)
                for n, t in enumerate(o_tiles(j)):
                    dve.wait_ge(vx_ready, t + 1)
                    if t >= 2:
                        dve.wait_ge(avT_ready, t - 1)
                    dve.tensor_tensor(av[:, n, :].rearrange("p (e r) -> p e r", r=RANK),
                                      b_z[:, n, :].rearrange("p (e r) -> p e r", r=RANK),
                                      alpha[:, n, :].unsqueeze(2).broadcast_to([P, EXPERTS, RANK]),
                                      ALU.mult).then_inc(av_done, 1)

            def evac_avT(t):
                n = t % 2
                dve.wait_ge(avT_hi, t + 1)
                dve.tensor_tensor(avT[1][n], avT_bank[n], avT[0][n].bitcast(F32), ALU.subtract).then_inc(avT_lo, 1)

            dve.wait_ge(p2_zeroed, 2)

            def sums2(p):
                dve.wait_ge(exp2_done, p + 1)
                dve.tensor_reduce(rs2[0:ROWS, p % 2, :], p2[p % 3][0:ROWS, :, 0:S], AX_X,
                                  ALU.add).then_inc(sum2_done, 1)

            def recip2(p):
                dve.wait_ge(sum2_done, p + 1)
                dve.reciprocal(rinv2[0:ROWS, p % 2, :], rs2[0:ROWS, p % 2, :]).then_inc(recip2_done, 1)

            def half_scores(half):
                return b_z[0:ROWS, half, :].rearrange("p (h m) -> p h m", m=SLOT)[:, :, 0:S]

            def max2(p, half):
                dve.wait_ge(s2_ready, 2 * p + half + 1)
                dve.tensor_reduce(mx2[0:ROWS, p % 2, 8 * half:8 * half + 8], half_scores(half), AX_X,
                                  ALU.max).then_inc(max2_done, 1)

            def sub2(p, half):
                heads = slice(8 * half, 8 * half + 8)
                if p >= 3:
                    dve.wait_ge(t2_ready, p - 2)
                dve.wait_ge(max2_done, 2 * p + half + 1)
                dve.tensor_tensor(p2[p % 3][0:ROWS, heads, 0:S], half_scores(half),
                                  mx2[0:ROWS, p % 2, heads].unsqueeze(2).broadcast_to([ROWS, 8, S]),
                                  ALU.subtract).then_inc(sub2_done, 1)

            def evac_z2_lo(p):
                dve.wait_ge(z2_hi, p + 1)
                cols = slice(p * 2 * S, (p + 1) * 2 * S)
                dve.tensor_tensor(z2[1][:, :, cols], z2_bank, z2[0][:, :, cols].bitcast(F32),
                                  ALU.subtract).then_inc(z2_lo, 1)

            def second_sums(j):
                t = o_tiles(j)
                a = acc[:, t.start:t.stop, :]
                dve.wait_ge(out2_ready, j + 1)
                dve.wait_ge(xT_ready, j + 1)
                dve.tensor_tensor(a, b_qk[1][:, 0:len(t) * D].rearrange("p (t d) -> p t d", d=D), a,
                                  ALU.add).then_inc(out2_added, 1)

            def second_moments(j):
                moments(1, j, (out2_added, j + 1))

            for u in range(PAIRS):
                if u == 2:
                    dve.wait_ge(w_lo[O_], 2 * NG + 2)
                max2(u, 0)
                max2(u, 1)
                sub2(u, 0)
                sub2(u, 1)
                if u >= 3:
                    evac_z2_lo(u - 3)
                if u >= 1:
                    sums2(u - 1)
                    recip2(u - 1)
                if (j := out2_after(u - 4)) is not None:
                    second_sums(j)
                    second_moments(j)
            evac_xT(4, x2)
            sums2(7)
            recip2(7)
            second_sums(1)
            evac_z2_lo(5)
            second_moments(1)
            softmax(0)
            evac_z2_lo(6)
            weigh(0)
            evac_xT(5, x2)
            evac_avT(0)
            evac_z2_lo(7)
            for j in (2, 3):
                second_sums(j)
                second_moments(j)
            evac_avT(1)
            softmax(1)
            weigh(1)
            evac_xT(6, x2)
            experts_out(0)
            evac_avT(2)
            evac_avT(3)
            softmax(2)
            weigh(2)
            evac_xT(7, x2)
            experts_out(1)
            evac_avT(4)
            evac_avT(5)
            softmax(3)
            weigh(3)
            evac_avT(6)
            experts_out(2)
            experts_out(3)
            normalize(2, 3)

        @block.tensor
        def _(pe):
            def three(out_, terms, start=True, stop=True, **kw):
                last = None
                steps = [(a, b) for (ah, al), (bh, bl) in terms for a, b in ((ah, bh), (al, bh), (ah, bl))]
                for n, (a, b) in enumerate(steps):
                    last = pe.matmul(out_, a, b, start=(start and n == 0), stop=(stop and n == len(steps) - 1), **kw)
                return last

            def qk(s, i, first=False, between=lambda c: None):
                for c in range(2):
                    batches = slice(c * NB // 2, (c + 1) * NB // 2)
                    for m in (Q_, K_):
                        if c == 0:
                            pe.wait_ge(w_lo[m], s + 1)
                        wh, wl = (qk_cols(m, i)(t) for t in (w_h, w_l))
                        if not first or c > 0:
                            pe.wait_ge(qk_evac, s * 4 + 2 * c + m - 1)
                        bank = b_qk[m][:, 0:HALF]
                        if first:
                            for k in range(KD):
                                if m == Q_:
                                    pe.wait_ge((x_hi_act, x_hi_dve)[k], c + 1)
                                for w in (wh, wl):
                                    pe.matmul(bank, w[:, k, :], xt_h[:, k, batches, 0:S],
                                              start=(k == 0 and w is wh), stop=False)
                            for k in range(KD):
                                if m == Q_:
                                    pe.wait_ge(x_lo, 2 * c + k + 1)
                                mm = pe.matmul(bank, wh[:, k, :], xt_l[:, k, batches, 0:S], start=False,
                                               stop=(k == KD - 1))
                        else:
                            mm = three(bank, [((wh[:, k, :], wl[:, k, :]),
                                               (xt_h[:, k, batches, 0:S], xt_l[:, k, batches, 0:S]))
                                              for k in range(KD)])
                        mm.then_inc(qk_ready, 1)
                    between(c)

            def transposes(s):
                pe.wait_ge(pn_ready, s + 1)
                for t in range(4):
                    mm = pe.transpose(b_t[0:ROWS, t * P:t * P + ROWS],
                                      probn[0:ROWS, 2 * t:2 * t + 2, :].rearrange("p a m -> p (a m)")[:, 0:ROWS],
                                      ident[0:ROWS, 0:ROWS])
                mm.then_inc(t_ready, 1)

            def scores(s, first=False):
                if not first:
                    pe.wait_ge(sub_done, s)
                pe.matmul(b_s.rearrange("p (a m) -> p a m", m=SLOT)[:, :, 0:S], ident_b[:], mask[:, :, 0:S],
                          start=True, stop=False, skip_group_check=True)
                for t, c, r in ((t, c, r) for t in range(4) for c in range(2) for r in range(2)):
                    b = 4 * t + 2 * r + c
                    if b == 0:
                        pe.wait_ge(qk_evac, s * 4 + 2)
                    if b == NB // 2:
                        pe.wait_ge(qk_evac, s * 4 + 4)
                    cols = slice(b * S, (b + 1) * S)
                    mm = pe.matmul(b_s[SLOT * r:SLOT * r + S, t * P + SLOT * c:t * P + SLOT * c + S],
                                   qT[:, cols], kT[:, cols], start=False, stop=True, skip_group_check=True)
                mm.then_inc(s_ready, 1)

            def pv(s, i, g, first=False):
                pe.wait_ge(pt_act, s + 1)
                pe.wait_ge(pt_dve, s + 1)
                pe.wait_ge(v_evac, (g + 1) * PAIRS)
                for c in range(2):
                    if not first:
                        pe.wait_ge(z_hi, s * 2 + c - 1)
                        pe.wait_ge(z_lo, s * 2 + c - 1)
                    for p in range(4):
                        pair = 4 * c + p
                        mm = pe.matmul(b_z[:, c, p * 2 * S:(p + 1) * 2 * S], v[0:ROWS, pair, i * E:(i + 1) * E],
                                       pT[0:ROWS, pair, :], start=True, stop=True)
                    mm.then_inc(z_ready, 1)

            def values(g):
                pe.wait_ge(w_hi[V_], 2 * g + 2)
                pe.wait_ge(w_lo[V_], 2 * g + 2)
                wh, wl = (t[:, V_, :].rearrange("p (k n) -> p k n", k=KD) for t in (w_h, w_l))
                for j in range(PAIRS):
                    if j >= 2:
                        pe.wait_ge(v_evac, g * PAIRS + j - 1)
                    xs = [tuple(t[:, k, 2 * j:2 * j + 2, :].rearrange("p b s -> p (b s)")[:, 0:ROWS]
                                for t in (xt_h, xt_l)) for k in range(KD)]
                    three(b_vo[j % 2][0:ROWS, :],
                          [(xs[k], (wh[:, k, :], wl[:, k, :])) for k in range(KD)]).then_inc(v_ready, 1)

            def project_heads(g, j, heads, first=True, last=True):
                wh, wl = (t[:, O_, :].rearrange("p (h n) -> p h n", h=G) for t in (w_h, w_l))
                for n, t in enumerate(o_tiles(j)):
                    cols = slice(t * P, (t + 1) * P)
                    whole = first and last
                    mm = three(b_vo[j % 2][:, n * D:(n + 1) * D],
                               [((z_h[:, h, cols], z_l[:, h, cols]), (wh[:, h, :], wl[:, h, :])) for h in heads],
                               start=first and (whole or n == 0), stop=last, skip_group_check=not whole)
                if last:
                    mm.then_inc(o_ready, 1)

            def project(g):
                pe.wait_ge(w_lo[O_], 2 * g + 2)
                pe.wait_ge(z_lo, (g + 1) * G * 2)
                for j in range(4):
                    if j < 2:
                        pe.wait_ge(v_evac, (g + 1) * PAIRS + PAIRS - 1 + j)
                    else:
                        pe.wait_ge(o_added, g * 4 + j - 1)
                    project_heads(g, j, range(G))

            pe.wait_ge(still_zero, 1)
            for _ in range(WARM_UP):
                pe.matmul(b_z[:, 0, :], still[:, 0:P], still[:], start=True, stop=True)

            def group(g, first=False):
                for i in range(G):
                    s = g * G + i
                    begin = first and i == 0
                    if first:
                        qk(s, i, begin, between=lambda c: [latent_keys(n) for n in ctx_uses(i)[c:c + 1]])
                    else:
                        qk(s, i, begin)
                    if begin:
                        pe.wait_ge(consts, 7)
                        pe.wait_ge(zeroed, 2)
                    else:
                        transposes(s - 1)
                    scores(s, begin)
                    if i == 0:
                        if not first:
                            pv(s - 1, G - 1, g - 1)
                        values(g)
                        if not first:
                            project(g - 1)
                    else:
                        pv(s - 1, i - 1, g, first and i == 1)

            def latent_keys(n):
                if n == 0:
                    pe.wait_ge(ctx_lo, 3)
                if n < 2:
                    pe.wait_ge(v_evac, PAIRS - 1 + n)
                else:
                    pe.wait_ge(keys_staged, n - 1)
                g, c = n % GP, n // GP
                batches = slice(1 + 8 * c, 1 + 8 * c + 8)
                pe.matmul(b_vo[n % 2][:, 0:HALF], wk_h[:, g, :], ctx_hl[:, batches, 0:S], start=True, stop=False)
                pe.matmul(b_vo[n % 2][:, 0:HALF], wk_l[:, g, :], ctx_hl[0:XL, batches, 0:S],
                          start=False, stop=True).then_inc(keys_ready, 1)

            def latent_values(n):
                if n == 5:
                    pe.wait_ge(o_added, NG * 4)
                elif n in (4, 6):
                    pe.wait_ge(values_placed, n - 1 if n == 4 else n)
                elif n == 7:
                    pe.wait_ge(q2_act, 3)
                for i in range(2):
                    b = 2 * n + i
                    hl, hi = (ctx_hl[0:k, b:b + 2, :].rearrange("p b m -> p (b m)")[:, 0:ROWS] for k in (P, XL))
                    dst = value_bank(n)[0:ROWS, i * D:(i + 1) * D]
                    pe.matmul(dst, hl, wv_h[:], start=True, stop=False)
                    mm = pe.matmul(dst, hi, wv_l[:], start=False, stop=True)
                mm.then_inc(values_ready, 1)

            group(0, first=True)
            pe.wait_ge(keys_staged, 4)
            with pe.Fori(1, NG) as g:
                group(g)

            pe.wait_ge(w_lo[O_], 2 * NG)
            pe.wait_ge(z_lo, (NH - 2) * 2)
            for j in range(2):
                project_heads(NG - 1, j, range(0, 2), last=False)
            transposes(NH - 1)
            latent_values(0)
            pv(NH - 1, G - 1, NG - 1)
            pe.wait_ge(z_lo, (NH - 1) * 2)
            for j in range(2):
                project_heads(NG - 1, j, range(2, 3), first=False, last=False)
            latent_values(1)

            def transpose_x(n):
                pe.wait_ge(*normalized(n))
                if n in (2, 3):
                    pe.wait_ge(xT_lo, n - 1)
                elif n > 4:
                    pe.wait_ge(lg_step, 2 * (n - 5) + 2)
                for i, t in enumerate(o_tiles(n % 4)):
                    for k in range(KD):
                        mm = pe.transpose(xT_bank(n)[:, k, i * P:(i + 1) * P],
                                          acc[:, t, k * P:(k + 1) * P], ident[:])
                mm.then_inc(xT_ready, 1)

            def queries(n):
                g, c = n % GP, n // GP
                pe.wait_ge(xT_lo, 2 * c + 2)
                if n >= 2:
                    pe.wait_ge(q2_act, n - 1)
                    pe.wait_ge(q2_dve, n - 1)
                cols = slice(c * HALF, (c + 1) * HALF)
                three(b_qk[n % 2][:, 0:HALF],
                      [(tuple(w[:, k, g * P:(g + 1) * P] for w in wq2), tuple(x[:, k, cols] for x in x1))
                       for k in range(KD)]).then_inc(q2_ready, 1)

            pe.wait_ge(z_lo, NH * 2)
            for j in range(2):
                project_heads(NG - 1, j, range(3, 4), first=False)
            latent_values(2)
            pe.wait_ge(o_added, NG * 4 - 3)
            project_heads(NG - 1, 2, range(G))
            transpose_x(0)
            pe.wait_ge(o_added, NG * 4 - 2)
            project_heads(NG - 1, 3, range(G))
            transpose_x(1)
            latent_values(3)
            latent_values(4)
            pe.wait_ge(w_lo[Q_], (NG + 1) * G)
            queries(0)
            queries(1)
            transpose_x(2)
            transpose_x(3)

            def scores2(p):
                if p == 0:
                    pe.wait_ge(values_placed, 5)
                pe.wait_ge(q2_act, 2 * (p // 4) + 2)
                pe.wait_ge(q2_dve, 2)
                for half in range(2):
                    if p > 0:
                        pe.wait_ge(sub2_done, 2 * p + half - 1)
                    pe.matmul(b_z[:, half, :].rearrange("p (a m) -> p a m", m=SLOT)[:, :, 0:S], ident_b[:],
                              mask[:, :, 0:S], start=True, stop=False, skip_group_check=True)
                    for y in range(2):
                        dst = b_z[0:ROWS, half, y * D:(y + 1) * D].rearrange("p (h m) -> p h m", m=SLOT)
                        mm = pe.matmul(dst[:, :, 0:S],
                                       q2[:, half, y, p, :], k2[:, half, y, p, :, :], start=False, stop=True,
                                       skip_group_check=True)
                    mm.then_inc(s2_ready, 1)

            def transposes2(p):
                pe.wait_ge(pn2_ready, p + 1)
                if p == 2:
                    pe.wait_ge(p2_zeroed, 3)
                if p > 0:
                    pe.wait_ge(t2_evac, p)
                for h in range(HP):
                    mm = pe.transpose(b_st[0:ROWS, h // 4, (h % 4) * P:(h % 4) * P + ROWS],
                                      p2[p % 3][0:ROWS, 2 * h:2 * h + 2, :].rearrange("p a m -> p (a m)")[:, 0:ROWS],
                                      ident[0:ROWS, 0:ROWS])
                mm.then_inc(t2_ready, 1)

            def pv2(p):
                pe.wait_ge(t2_evac, p + 1)
                pe.wait_ge(values_placed, min(p + 2, 8))
                if p > 0:
                    pe.wait_ge(z2_lo, p)
                for k, r, q in ((k, r, q) for k in range(KD) for r in range(2) for q in range(4)):
                    h = 4 * k + q
                    place = h ^ (HG // 2) if r == 1 else h
                    mm = pe.matmul(z2_bank[q * 2 * XE:(q + 1) * 2 * XE, k, r * S:(r + 1) * S],
                                   v2[0:ROWS, 2 * p + r, h, :], pT2[p % 2][0:ROWS, place, SLOT * r:SLOT * r + S],
                                   start=True, stop=True)
                mm.then_inc(z2_ready, 1)

            def out2(p, j):
                pe.wait_ge(z2_lo, p + 1)
                if j > 0:
                    pe.wait_ge(out2_added, j)
                for i, t in enumerate(o_tiles(j)):
                    cols = slice(t * P, (t + 1) * P)
                    mm = three(b_qk[1][:, i * D:(i + 1) * D],
                               [(tuple(z[:, k, cols] for z in z2), tuple(w[:, k, :] for w in wout))
                                for k in range(KD)])
                mm.then_inc(out2_ready, 1)

            def hidden(j):
                tiles = o_tiles(j)
                cols = slice(tiles.start * P, tiles.stop * P)
                pe.wait_ge(xT_lo, 4 + j + 1)
                for m in range(KD):
                    mm = three(b_vo[1][:, m * D:m * D + len(tiles) * P],
                               [(tuple(w[:, k, m * P:(m + 1) * P] for w in w1), tuple(x[:, k, cols] for x in x2))
                                for k in range(KD)])
                mm.then_inc(h_ready, 1)

            def ranks(t):
                if t >= 2:
                    pe.wait_ge(av_done, t - 1)
                three(b_z[:, t % 2, :], [(tuple(x[:, k, t * P:(t + 1) * P] for x in x2),
                                          tuple(w[:, k, :] for w in vw)) for k in range(KD)]).then_inc(vx_ready, 1)

            def logits(j):
                pe.wait_ge(h_evac, j + 1)
                cols = slice(0, len(o_tiles(j)) * P)
                for k in range(KD):
                    mm = pe.matmul(b_vo[1][0:EXPERTS, cols], w2_s[:, k, :], hT[:, k, cols], start=(k == 0),
                                   stop=(k == KD - 1))
                mm.then_inc(lgT_ready, 1)

            def transpose_logits(j):
                pe.wait_ge(lgT_evac, j + 1)
                for n in range(len(o_tiles(j))):
                    mm = pe.transpose(b_vo[1][:, 2 * P + n * EXPERTS:2 * P + (n + 1) * EXPERTS],
                                      lgT[:, n * P:(n + 1) * P], ident[0:EXPERTS, 0:EXPERTS])
                mm.then_inc(lg_ready, 1)

            def transpose_av(t):
                pe.wait_ge(av_done, t + 1)
                if t >= 2:
                    pe.wait_ge(avT_lo, t - 1)
                for c in range(KR):
                    mm = pe.transpose(avT_bank[t % 2][:, c, :], av[:, t % 2, c * P:(c + 1) * P], ident[:])
                mm.then_inc(avT_ready, 1)

            def experts(t):
                j, n = t // 2, t % 2
                if n == 0 and j >= 2:
                    pe.wait_ge(u_added, j - 1)
                pe.wait_ge(avT_lo, t + 1)
                mm = three(b_st[:, j % 2, n * D:(n + 1) * D],
                           [(tuple(a[n][:, c, :] for a in avT), tuple(w[:, c, :] for w in uw)) for c in range(KR)])
                if t + 1 == o_tiles(j).stop:
                    mm.then_inc(u_ready, 1)

            pe.wait_ge(w_lo[K_], (NG + 1) * G)
            pe.wait_ge(k2_dve, 8)
            pe.wait_ge(k2_pool, 8)
            for u in range(PAIRS):
                scores2(u)
                if u < 2:
                    queries(2 + u)
                if u == 1:
                    latent_values(5)
                if u == 2:
                    latent_values(6)
                if u >= 3:
                    pv2(u - 3)
                if (j := out2_after(u - 4)) is not None:
                    out2(u - 4, j)
                if u >= 2:
                    transposes2(u - 2)
            pe.wait_ge(d_small, 48)
            latent_values(7)
            pe.wait_ge(values_placed, 7)
            transpose_x(4)
            out2(4, 1)
            pv2(5)
            hidden(0)
            transposes2(6)
            pe.wait_ge(sub2_done, 2 * PAIRS)
            pe.wait_ge(w_lo[V_], 2 * NG + 2)
            ranks(0)
            logits(0)
            transposes2(7)
            transpose_logits(0)
            pv2(6)
            ranks(1)
            transpose_x(5)
            pe.wait_ge(values_placed, 8)
            transpose_av(0)
            pv2(7)
            hidden(1)
            out2(6, 2)
            ranks(2)
            out2(7, 3)
            pe.wait_ge(z2_lo, PAIRS)
            transpose_av(1)
            pe.wait_ge(t2_evac, PAIRS)
            pe.wait_ge(w_lo[O_], 2 * NG + 2)
            experts(0)
            logits(1)
            ranks(3)
            transpose_logits(1)
            experts(1)
            transpose_x(6)
            transpose_av(2)
            transpose_av(3)
            hidden(2)
            ranks(4)
            logits(2)
            experts(2)
            transpose_logits(2)
            ranks(5)
            transpose_x(7)
            experts(3)
            hidden(3)
            transpose_av(4)
            logits(3)
            transpose_av(5)
            transpose_logits(3)
            ranks(6)
            experts(4)
            transpose_av(6)
            experts(5)
            experts(6)


def lay_out(inputs):
    import numpy as np
    a = {k: np.asarray(v) for k, v in inputs.items()}
    w = np.zeros((NG + 1, 4, P, W), np.float32)
    for m, name in ((Q_, "L0_attn_W_Q"), (K_, "L0_attn_W_K"), (V_, "L0_attn_W_V")):
        w[:NG, m] = a[name].reshape(NG, G, E, KD, P).transpose(0, 4, 3, 1, 2).reshape(NG, P, W)
    w[:NG, O_] = a["L0_attn_W_O"].reshape(NG, G, D, E).transpose(0, 3, 1, 2).reshape(NG, P, W)
    w[NG, Q_].reshape(P, KD, 2 * D)[:, :, 0:D] = a["L0_xattn_Wq"].reshape(D, KD, P).transpose(2, 1, 0)
    wo = a["L0_xattn_Wout"].reshape(D, KD, P).transpose(2, 1, 0)
    w1 = a["L0_ffn_W1"].reshape(KD, P, D).transpose(1, 0, 2)
    w[NG, K_] = np.concatenate([wo, w1], axis=2).reshape(P, W)
    w[NG, V_] = a["L0_ffn_V"].reshape(EXPERTS * RANK, KD, P).transpose(2, 1, 0).reshape(P, W)
    w[NG, O_] = a["L0_ffn_U"].transpose(0, 2, 1).reshape(KR, P, D).transpose(1, 0, 2).reshape(P, W)
    wk, wv = a["L0_xattn_Wkv_expand"].reshape(2, D, XL)
    return {
        "x": a["x"].reshape(N, D),
        "xT": a["x"].transpose(2, 0, 1),
        "weights": w,
        "ctxT": np.concatenate([a["ctx_512"][NB - 1:, 0:S], a["ctx_512"][:, 0:S]]).transpose(2, 0, 1),
        "wk": np.tile(wk.T.reshape(XL, GP, P), (2, 1, 1)),
        "wv": np.tile(wv.T, (2, 1)),
        "w2": a["L0_ffn_W2"].reshape(KD, P, EXPERTS).transpose(1, 0, 2),
        "b1": a["L0_ffn_b1"].reshape(KD, P).T,
        "b2": a["L0_ffn_b2"].reshape(EXPERTS, 1),
    }


def kernel(**inputs):
    import numpy as np
    import concourse.bacc as bacc
    from concourse.bass_utils import run_bass_kernel_spmd

    nc = bacc.Bacc("TRN2", target_bir_lowering=False, num_devices=1)
    arrays = {n: np.ascontiguousarray(a) for n, a in lay_out(inputs).items()}
    aps = {n: nc.dram_tensor(n, a.shape, mybir.dt.from_np(a.dtype), kind="ExternalInput").ap()
           for n, a in arrays.items()}
    out = nc.dram_tensor("out", (N, D), F32, kind="ExternalOutput").ap()
    build(nc, out=out, **aps)
    r = run_bass_kernel_spmd(nc, [arrays], core_ids=[0])
    return r.results[0]["out"].reshape(NB, S, D)
```
